# Optimizing a Trainium2 kernel written in Bass

```python
import numpy as np
import jax
import jax.numpy as jnp

def _softmax(x, axis=-1):
    return jax.nn.softmax(x, axis=axis)

def _gelu(x):
    return jax.nn.gelu(x, approximate=True)

def _silu(x):
    return jax.nn.silu(x)

def _sigmoid(x):
    return jax.nn.sigmoid(x)

def _layernorm(x, axis=-1, eps=1e-05):
    m = jnp.mean(x, axis=axis, keepdims=True)
    v = jnp.var(x, axis=axis, keepdims=True)
    return (x - m) / jnp.sqrt(v + eps)

def _scatter_add(tgt, idx, src, axis=0):
    return tgt.at[idx].add(src)

def _segment_sum(src, seg, n):
    return jax.ops.segment_sum(src, seg, n)
kernel_name = 'mk_adaln_ffn_d2_seqx_r4_91ae7b'

def setup_inputs(seed: int=0):
    np.random.seed(seed)
    _w = jnp.asarray

    def _rec_inputs():
        import jax
        import jax.numpy as jnp
        _rk = jax.random.key(seed)
        x = -0.000125 + 0.9999 * jax.random.normal(jax.random.fold_in(_rk, 1), (32, 64, 1024), jnp.float32)
        _lenS = 64 - jax.random.randint(jax.random.fold_in(_rk, 7), (32,), 0, max(1, 64 // 4) + 1, jnp.int32)
        _lenS2 = 64 - jax.random.randint(jax.random.fold_in(_rk, 8), (32,), 0, max(1, 64 // 4) + 1, jnp.int32)
        cond_128 = 0.0061147 + 1.02565 * jax.random.normal(jax.random.fold_in(_rk, 11), (32, 128), jnp.float32)
        fside_S_0 = -0.022604 + 0.987366 * jax.random.normal(jax.random.fold_in(_rk, 12), (64,), jnp.float32)
        return (x, cond_128, fside_S_0)
    x, cond_128, fside_S_0 = _rec_inputs()

    def _L0_cond_setup():
        import jax, jax.numpy as jnp
        import numpy as np
        from jax import lax
        N, C_IN, L = (32, 64, 1024)
        C_OUT, K, GROUPS = (64, 9, 4)
        C_DIM, PAD, STRIDE = (128, 4, 1)
        key = jax.random.key(seed)
        k1, k2, k3, k4, k5 = jax.random.split(key, 5)
        x = jax.random.normal(k1, (N, C_IN, L), dtype=jnp.float32)
        c = jax.random.normal(k2, (N, C_DIM), dtype=jnp.float32)
        weight = jax.random.normal(k3, (C_OUT, C_IN // GROUPS, K), dtype=jnp.float32)
        c_weight = jax.random.normal(k4, (C_OUT, C_DIM), dtype=jnp.float32)
        bias = jax.random.normal(k5, (C_OUT,), dtype=jnp.float32)
        return {'x': x, 'c': c, 'weight': weight, 'c_weight': c_weight, 'bias': bias}
    _L0_cond_all = _L0_cond_setup()
    _L0_cond_in = {k: v for k, v in _L0_cond_all.items() if k in ('weight', 'c_weight')}
    del _L0_cond_all

    def _L0_ffn_setup():
        import jax, jax.numpy as jnp
        import numpy as np
        RANKS = (8, 16, 32, 64)
        TOPK = 1
        SCALING = 1.0 / 4
        key = jax.random.key(seed)
        ks = jax.random.split(key, 7)
        D_IN, D_OUT, MAX_R, N_RANKS = (1024, 1024, 64, len(RANKS))
        B_, S_ = (4, 512)
        return {'hidden_states': jax.random.normal(ks[0], (B_, S_, D_IN), jnp.float32), 'W': jax.random.normal(ks[1], (D_OUT, D_IN), jnp.float32) * 0.02, 'b': jax.random.normal(ks[2], (D_OUT,), jnp.float32) * 0.02, 'A': jax.random.normal(ks[3], (MAX_R, D_IN), jnp.float32) * 0.02, 'B': jnp.zeros((D_OUT, MAX_R), jnp.float32) + jax.random.normal(ks[4], (D_OUT, MAX_R), jnp.float32) * 0.02, 'gate_w': jax.random.normal(ks[5], (N_RANKS, D_IN), jnp.float32) * 0.02, 'gate_b': jax.random.normal(ks[6], (N_RANKS,), jnp.float32) * 0.02}
    _L0_ffn_all = _L0_ffn_setup()
    _L0_ffn_in = {k: v for k, v in _L0_ffn_all.items() if k in ('W', 'b', 'A', 'B', 'gate_w', 'gate_b')}
    del _L0_ffn_all

    def _L1_cond_setup():
        import jax, jax.numpy as jnp
        import numpy as np
        K = 8
        T = 1.0
        D_EMBD = 128
        IN_C = 64
        OUT_C = 64
        BS = 32
        H = 1024
        HID = 128
        key = jax.random.key(seed)
        ks = jax.random.split(key, 10)
        s = lambda fan_in: 1.0 / np.sqrt(fan_in)
        return {'x': jax.random.normal(ks[0], (BS, IN_C, H), dtype=jnp.float32), 'embedding': jax.random.normal(ks[1], (BS, D_EMBD), dtype=jnp.float32), 'W0': jax.random.normal(ks[2], (D_EMBD, HID), dtype=jnp.float32) * s(D_EMBD), 'b0': jnp.zeros((HID,), dtype=jnp.float32), 'W1': jax.random.normal(ks[3], (HID, HID), dtype=jnp.float32) * s(HID), 'b1': jnp.zeros((HID,), dtype=jnp.float32), 'W2': jax.random.normal(ks[4], (HID, K), dtype=jnp.float32) * s(HID), 'b2': jnp.zeros((K,), dtype=jnp.float32), 'weight': jax.random.normal(ks[5], (K, OUT_C, IN_C, 1), dtype=jnp.float32) * s(IN_C), 'bias_k': jax.random.normal(ks[6], (K, OUT_C), dtype=jnp.float32) * 0.1}
    _L1_cond_all = _L1_cond_setup()
    _L1_cond_in = {k: v for k, v in _L1_cond_all.items() if k in ('W0', 'b0', 'W1', 'b1', 'W2', 'b2', 'weight', 'bias_k')}
    del _L1_cond_all

    def _L1_ffn_setup():
        import jax, jax.numpy as jnp
        import numpy as np

        def sparsemax(z):
            E = z.shape[-1]
            z_sorted = -jnp.sort(-z, axis=-1)
            z_cum = jnp.cumsum(z_sorted, axis=-1)
            k = jnp.arange(1, E + 1, dtype=z.dtype)
            support = 1.0 + k * z_sorted > z_cum
            k_z = jnp.sum(support, axis=-1, keepdims=True)
            tau_sum = jnp.take_along_axis(z_cum, k_z.astype(jnp.int32) - 1, axis=-1)
            tau = (tau_sum - 1.0) / k_z.astype(z.dtype)
            return jnp.maximum(z - tau, 0.0)
        key = jax.random.key(seed)
        ks = jax.random.split(key, 6)
        B, S, D_IN, D_OUT, E, R = (8, 512, 1024, 1024, 8, 16)
        x = jax.random.normal(ks[0], (B, S, D_IN), dtype=jnp.float32)
        W_base = jax.random.normal(ks[1], (D_OUT, D_IN), dtype=jnp.float32) * D_IN ** (-0.5)
        b_base = jax.random.normal(ks[2], (D_OUT,), dtype=jnp.float32) * 0.01
        W_router = jax.random.normal(ks[3], (E, D_IN), dtype=jnp.float32) * D_IN ** (-0.5)
        b_router = jnp.zeros((E,), dtype=jnp.float32)
        lora_A = jax.random.normal(ks[4], (E, D_IN, R), dtype=jnp.float32) * D_IN ** (-0.5)
        lora_B = jnp.zeros((E, R, D_OUT), dtype=jnp.float32)
        return {'x': x, 'W_base': W_base, 'b_base': b_base, 'W_router': W_router, 'b_router': b_router, 'lora_A': lora_A, 'lora_B': lora_B}
    _L1_ffn_all = _L1_ffn_setup()
    _L1_ffn_in = {k: v for k, v in _L1_ffn_all.items() if k in ('W_base', 'b_base', 'W_router', 'b_router', 'lora_A', 'lora_B')}
    del _L1_ffn_all
    return {'x': x, 'cond_128': cond_128, 'fside_S_0': fside_S_0, 'L0_cond_weight': _L0_cond_in['weight'], 'L0_cond_c_weight': _L0_cond_in['c_weight'], 'L0_ffn_W': _L0_ffn_in['W'], 'L0_ffn_b': _L0_ffn_in['b'], 'L0_ffn_A': _L0_ffn_in['A'], 'L0_ffn_B': _L0_ffn_in['B'], 'L0_ffn_gate_w': _L0_ffn_in['gate_w'], 'L0_ffn_gate_b': _L0_ffn_in['gate_b'], 'L1_cond_W0': _L1_cond_in['W0'], 'L1_cond_b0': _L1_cond_in['b0'], 'L1_cond_W1': _L1_cond_in['W1'], 'L1_cond_b1': _L1_cond_in['b1'], 'L1_cond_W2': _L1_cond_in['W2'], 'L1_cond_b2': _L1_cond_in['b2'], 'L1_cond_weight': _L1_cond_in['weight'], 'L1_cond_bias_k': _L1_cond_in['bias_k'], 'L1_ffn_W_base': _L1_ffn_in['W_base'], 'L1_ffn_b_base': _L1_ffn_in['b_base'], 'L1_ffn_W_router': _L1_ffn_in['W_router'], 'L1_ffn_b_router': _L1_ffn_in['b_router'], 'L1_ffn_lora_A': _L1_ffn_in['lora_A'], 'L1_ffn_lora_B': _L1_ffn_in['lora_B']}

def reference(x, cond_128, fside_S_0, L0_cond_weight, L0_cond_c_weight, L0_ffn_W, L0_ffn_b, L0_ffn_A, L0_ffn_B, L0_ffn_gate_w, L0_ffn_gate_b, L1_cond_W0, L1_cond_b0, L1_cond_W1, L1_cond_b1, L1_cond_W2, L1_cond_b2, L1_cond_weight, L1_cond_bias_k, L1_ffn_W_base, L1_ffn_b_base, L1_ffn_W_router, L1_ffn_b_router, L1_ffn_lora_A, L1_ffn_lora_B):
    import jax
    import jax.numpy as jnp

    def _L0_cond_ref(x, c, weight, c_weight, bias):
        import jax, jax.numpy as jnp
        import numpy as np
        from jax import lax
        N, C_IN, L = (32, 64, 1024)
        C_OUT, K, GROUPS = (64, 9, 4)
        C_DIM, PAD, STRIDE = (128, 4, 1)
        out = lax.conv_general_dilated(x, weight, window_strides=(STRIDE,), padding=[(PAD, PAD)], dimension_numbers=('NCH', 'OIH', 'NCH'), feature_group_count=GROUPS)
        ctx = jnp.einsum('nd,od->no', c, c_weight)
        out = out + ctx[:, :, None] + bias[None, :, None]
        return out

    def _L0_ffn_ref(hidden_states, W, b, A, B, gate_w, gate_b):
        import jax, jax.numpy as jnp
        import numpy as np
        RANKS = (8, 16, 32, 64)
        TOPK = 1
        SCALING = 1.0 / 4
        bsz, seq, d_in = hidden_states.shape
        out = jnp.einsum('bsd,od->bso', hidden_states, W) + b
        x = hidden_states.reshape(-1, d_in)
        scores = x @ gate_w.T + gate_b
        probs = jax.nn.softmax(scores, axis=-1)
        routing_weights, selected = jax.lax.top_k(probs, TOPK)
        routing_weights = routing_weights / jnp.sum(routing_weights, axis=-1, keepdims=True)
        lora_outputs = jnp.stack([x @ A[:r, :].T @ B[:, :r].T for r in RANKS], axis=1)
        sel = jnp.take_along_axis(lora_outputs, selected[:, :, None], axis=1)
        final = jnp.sum(sel * routing_weights[:, :, None], axis=1)
        return out + final.reshape(bsz, seq, -1)

    def _L1_cond_ref(x, embedding, W0, b0, W1, b1, W2, b2, weight, bias_k):
        import jax, jax.numpy as jnp
        import numpy as np
        K = 8
        T = 1.0
        D_EMBD = 128
        IN_C = 64
        OUT_C = 64
        BS = 32
        H = 1024
        HID = 128
        h = jax.nn.gelu(embedding @ W0 + b0, approximate=False)
        h = jax.nn.gelu(h @ W1 + b1, approximate=False)
        att = jax.nn.softmax((h @ W2 + b2) / T, axis=-1)
        agg_w = jnp.einsum('bk,koi->boi', att, weight[..., 0])
        agg_b = att @ bias_k
        out = jnp.einsum('boi,bih->boh', agg_w, x) + agg_b[:, :, None]
        return out

    def _L1_ffn_ref(x, W_base, b_base, W_router, b_router, lora_A, lora_B):
        import jax, jax.numpy as jnp
        import numpy as np

        def sparsemax(z):
            E = z.shape[-1]
            z_sorted = -jnp.sort(-z, axis=-1)
            z_cum = jnp.cumsum(z_sorted, axis=-1)
            k = jnp.arange(1, E + 1, dtype=z.dtype)
            support = 1.0 + k * z_sorted > z_cum
            k_z = jnp.sum(support, axis=-1, keepdims=True)
            tau_sum = jnp.take_along_axis(z_cum, k_z.astype(jnp.int32) - 1, axis=-1)
            tau = (tau_sum - 1.0) / k_z.astype(z.dtype)
            return jnp.maximum(z - tau, 0.0)
        base_out = jnp.einsum('bsd,od->bso', x, W_base) + b_base
        logits = jnp.einsum('bsd,ed->bse', x, W_router) + b_router
        weights = sparsemax(logits)
        h = jnp.einsum('bsd,edr->bser', x, lora_A)
        expert_out = jnp.einsum('bser,bse,ero->bso', h, weights, lora_B)
        return base_out + expert_out
    x = x + _L0_ffn_ref(_L0_cond_ref(x, cond_128, L0_cond_weight, L0_cond_c_weight, fside_S_0), L0_ffn_W, L0_ffn_b, L0_ffn_A, L0_ffn_B, L0_ffn_gate_w, L0_ffn_gate_b)
    x = x + _L1_ffn_ref(_L1_cond_ref(x, cond_128, L1_cond_W0, L1_cond_b0, L1_cond_W1, L1_cond_b1, L1_cond_W2, L1_cond_b2, L1_cond_weight, L1_cond_bias_k), L1_ffn_W_base, L1_ffn_b_base, L1_ffn_W_router, L1_ffn_b_router, L1_ffn_lora_A, L1_ffn_lora_B)
    return x

_drawn_inputs = setup_inputs


def setup_inputs(seed=0):
    import zlib

    import numpy as np

    out = dict(_drawn_inputs(seed))
    spreads = {'L1_cond_b0': (0.0, 0.473),
     'L1_cond_b1': (0.0, 0.334),
     'L1_cond_b2': (0.0, 0.276),
     'L1_ffn_b_router': (0.0, 0.8),
     'L1_ffn_lora_B': (0.0, 0.1)}
    factors = {'L0_ffn_b': 28.623, 'L0_ffn_gate_b': 40.536, 'L1_cond_bias_k': 8.0, 'L1_ffn_b_base': 64.0}
    for name, (base, spread) in spreads.items():
        noise = np.random.default_rng([zlib.crc32(name.encode()), seed]).standard_normal(out[name].shape)
        drawn = base * np.exp(spread * noise) if base else spread * noise
        out[name] = jnp.asarray(drawn.astype(out[name].dtype))
    for name, factor in factors.items():
        out[name] = (out[name] * factor).astype(out[name].dtype)
    return out
```

```python
from contextlib import ExitStack

import numpy as np

import concourse.bass as bass
from concourse import mybir

F32 = mybir.dt.float32
F32R = mybir.dt.float32r
ALU = mybir.AluOpType
ACT = mybir.ActivationFunctionType
AX_X = mybir.AxisListType.X

P = 128
NB, CH, D = 32, 64, 1024
TILES = NB * CH // P
NCH = D // P
HALF = D // 2
GROUPS, TAPS, PAD = 4, 9, 4
GC = CH // GROUPS
POS = P // GC
QB = D // POS
QX = QB + 1
TOEP = 2 * POS + POS - 1
RANK = 64
RANKS = (8, 16, 32, 64)
HID0 = RANK + len(RANKS)
EXP, ER = 8, 16
HID1 = EXP * ER + EXP
W0COLS, W1COLS = D + HID0, D + HID1
RAW = 6
KMIX = 8
OQ = CH // 4
EMB = 128

PK_C, PK_CW, PK_W0, PK_W1, PK_W2, PK_B0, PK_B1 = 0, 32, 96, 224, 352, 360, 361
PACK = 362
RW_FS, RW_GB, RW_B2, RW_RB = 0, 64, 68, 76
ROW = 84


def build(nc, x, xblk, toep, wcat0, bcat0, wcat1, bcat1, b_base, pack, rows, mixw, bias_k, out):
    x_t = x.rearrange("(t n) c h -> t (n c) h", n=2)
    out_t = out.rearrange("(t n) c h -> t (n c) h", n=2)
    x1_t = nc.dram_tensor("x1_scratch", (TILES, P, D), F32, kind="Internal").ap()

    with ExitStack() as ctx:
        def sb(name, shape, dt=F32):
            return ctx.enter_context(nc.sbuf_tensor(name, shape, dt))

        def psum(name, shape):
            return ctx.enter_context(nc.psum_tensor(name, shape, F32))

        def sem(name):
            return ctx.enter_context(nc.semaphore(name))

        w_hi = sb("w_hi", [P, NCH, W1COLS], F32R)
        w_lo = sb("w_lo", [P, NCH, W1COLS], F32R)
        w_raw = sb("w_raw", [P, RAW, W1COLS])
        lb_hi = sb("lb_hi", [P, D], F32R)
        lb_lo = sb("lb_lo", [P, D], F32R)
        lb_raw = sb("lb_raw", [P, D])
        toep_hi = sb("toep_hi", [P, GROUPS, 2 * P], F32R)
        toep_lo = sb("toep_lo", [P, GROUPS, 2 * P], F32R)
        agg_hi = sb("agg_hi", [P, TILES, 2, CH], F32R)
        agg_lo = sb("agg_lo", [P, TILES, 2, CH], F32R)
        ctx_row = sb("ctx_row", [P, TILES, P])
        aggb_row = sb("aggb_row", [P, TILES, P])
        bbase = sb("bbase", [P, D])
        x_buf = sb("x_buf", [P, 2, D])
        xs = [x_buf[:, 0, :], x_buf[:, 1, :]]
        blk_raw = sb("blk_raw", [P, 2 * GROUPS * QX])
        src_hi = sb("src_hi", [P, 2 * GROUPS * QX], F32R)
        src_lo = sb("src_lo", [P, 2 * GROUPS * QX], F32R)
        mixed = sb("mixed", [P, NCH, P])
        act_hi = sb("act_hi", [P, 2, NCH, P], F32R)
        act_lo = sb("act_lo", [P, 2, NCH, P], F32R)
        u_sb = sb("u_sb", [P, P])
        ut_hi = sb("ut_hi", [P, P], F32R)
        ut_lo = sb("ut_lo", [P, P], F32R)
        pk = sb("pk", [P, PACK])
        rw = sb("rw", [P, ROW])
        bk = sb("bk", [KMIX, CH])
        ident = sb("ident", [P, P])
        ones = sb("ones", [P, P])
        inv_k = sb("inv_k", [P, EXP])
        hg = sb("hg", [P, 2, NB])
        att = sb("att", [NB, 4, KMIX])
        stat = sb("stat", [NB, 4])
        attT = sb("attT", [P, NB])
        sc = sb("sc", [P, 8])
        pm = sb("pm", [P, 8])
        keep = sb("keep", [P, 4])
        kw = sb("kw", [P, 8])
        ex = sb("ex", [P, 4])
        st = sb("st", [P, 8])
        gs = sb("gs", [P, 4, EXP])

        acc = psum("acc", [P, 2, 2, HALF])
        mixp = psum("mixp", [P, 2, HALF])
        hidp = psum("hidp", [P, HALF])
        utp = psum("utp", [P, HALF])
        agg_ps = acc[:, 1, :, :].rearrange("p h (o b) -> p (h o) b", b=NB)

        s_pk = sem("s_pk")
        s_rw = sem("s_rw")
        s_bk = sem("s_bk")
        s_mixw = sem("s_mixw")
        s_bbase = sem("s_bbase")
        s_toep = sem("s_toep")
        s_lb = sem("s_lb")
        w_loaded = [sem(f"w_loaded{k}") for k in range(RAW)]
        src_loaded = sem("src_loaded")
        xs_loaded = [sem("xs_loaded0"), sem("xs_loaded1")]
        x1_loaded = [sem("x1_loaded0"), sem("x1_loaded1")]
        x1_stored = [sem("x1_stored0"), sem("x1_stored1")]
        out_stored = [sem("out_stored0"), sem("out_stored1")]
        whi_done = sem("whi_done")
        wlo_done = sem("wlo_done")
        lbhi_done = sem("lbhi_done")
        lblo_done = sem("lblo_done")
        toephi_done = sem("toephi_done")
        toeplo_done = sem("toeplo_done")
        srchi_done = sem("srchi_done")
        srclo_done = sem("srclo_done")
        acthi_done = sem("acthi_done")
        actlo_done = sem("actlo_done")
        uthi_done = sem("uthi_done")
        utlo_done = sem("utlo_done")
        mix_done = sem("mix_done")
        sum_done = sem("sum_done")
        hid_done = sem("hid_done")
        gate_op = sem("gate_op")
        gate_max = sem("gate_max")
        exp_done = sem("exp_done")
        gated = sem("gated")
        ut_done = sem("ut_done")
        half_done = [sem("half_done0"), sem("half_done1")]
        biased = sem("biased")
        res_done = [sem("res_done0"), sem("res_done1")]
        w_free = sem("w_free")
        consts = sem("consts")
        ident_zero = sem("ident_zero")
        ctx_prod = sem("ctx_prod")
        ctx_mm = sem("ctx_mm")
        ctx_ready = sem("ctx_ready")
        mlp_mm = sem("mlp_mm")
        mlp_h = sem("mlp_h")
        att_op = sem("att_op")
        att_exp = sem("att_exp")
        att_t = sem("att_t")
        att_copied = sem("att_copied")
        aggb_prod = sem("aggb_prod")
        agg_mm = sem("agg_mm")
        agghi_done = sem("agghi_done")
        agglo_done = sem("agglo_done")
        aggb_mm = sem("aggb_mm")
        aggb_done = sem("aggb_done")

        block = ctx.enter_context(nc.Block())
        LAST = 2 * TILES - 1
        GATE0, GATE1 = 9, 6

        def hi(part):
            return part.bitcast(F32)

        def mixw_at(j):
            return x_buf[32 * j:32 * j + KMIX, :, :].rearrange("k a (o n i) -> k (a o) n i", n=2, i=CH)

        def x1_slot(s):
            return blk_raw[:, 0:D] if s == 0 else xs[0][:, :]

        def loop_steps(eng, first, count, body):
            with eng.Fori(0, count // 2) as i:
                body(2 * i + first, 1)
                body(2 * i + (first + 1), 0)

        @block.sync
        def _(sp):
            def load_blocks(t):
                sp.dma_start(blk_raw[:, :], xblk[bass.ds(t, 1)].rearrange("a p n -> (a p) n")).then_inc(src_loaded, 16)

            def load_w(j):
                wcat, k, cols = (wcat0, j, W0COLS) if j < NCH else (wcat1, j - NCH, W1COLS)
                sp.dma_start(w_raw[:, j % RAW, 0:cols], wcat[:, k, :]).then_inc(w_loaded[j % RAW], 16)

            def load_x(t, s):
                sp.dma_start(xs[s][:, :], x_t[bass.ds(t, 1)].rearrange("a p h -> (a p) h")).then_inc(xs_loaded[s], 16)

            def load_x1(t, s):
                sp.dma_start(x1_slot(s), x1_t[bass.ds(t, 1)].rearrange("a p h -> (a p) h")).then_inc(x1_loaded[s], 16)

            def store_x1(t, s):
                sp.wait_ge(res_done[0], t + 1)
                sp.wait_ge(res_done[1], t + 1)
                sp.dma_start(x1_t[bass.ds(t, 1)].rearrange("a p h -> (a p) h"), xs[s][:, :]).then_inc(x1_stored[s], 16)

            def store_out(T, h):
                sp.wait_ge(res_done[h], T + 1)
                sp.dma_start(out_t[bass.ds(T - TILES, 1), :, h * HALF:(h + 1) * HALF].rearrange("a p h -> (a p) h"),
                             xs[1][:, h * HALF:(h + 1) * HALF]).then_inc(out_stored[h], 16)

            load_blocks(0)
            for j in range(3):
                load_w(j)
            sp.wait_ge(srclo_done, 1)
            load_blocks(1)
            for j in range(3, RAW):
                load_w(j)
            sp.dma_start(bbase[:, :], b_base.partition_broadcast(P)).then_inc(s_bbase, 16)
            for j in range(RAW, NCH):
                sp.wait_ge(wlo_done, j - RAW + 1)
                load_w(j)
            sp.wait_ge(agg_mm, 2)
            load_x(0, 0)
            load_x(1, 1)

            sp.wait_ge(srclo_done, 2)
            load_blocks(2)
            for j in range(NCH, NCH + RAW):
                sp.wait_ge(wlo_done, j - RAW + 1)
                load_w(j)
            sp.wait_ge(lblo_done, 1)
            sp.dma_start(lb_raw[:, :], bcat1).then_inc(s_lb, 16)

            def step0(T, s):
                store_x1(T - 1, 1 - s)
                sp.wait_ge(srclo_done, T + 2)
                load_blocks(T + 2)

            def next_x(T, s, stored):
                sp.wait_ge(x1_stored[1 - s], stored)
                load_x(T + 1, 1 - s)

            with sp.Fori(0, (TILES - 4) // 2) as i:
                step0(2 * i + 1, 1)
                next_x(2 * i + 1, 1, 16 * i + 16)
                step0(2 * i + 2, 0)
                next_x(2 * i + 2, 0, 16 * i + 16)
            T = TILES - 3
            step0(T, 1)
            next_x(T, 1, 16 * ((T - 1) // 2 + 1))
            T = TILES - 2
            store_x1(T - 1, 1)
            sp.wait_ge(srclo_done, TILES)
            sp.wait_ge(x1_stored[0], 16)
            load_x1(0, 0)
            next_x(T, 0, 16 * ((T - 1) // 2 + 1))
            store_x1(TILES - 2, 0)
            sp.wait_ge(x1_stored[0], 16 * (TILES // 2))
            sp.wait_ge(x1_stored[1], 16)
            load_x1(1, 1)
            for j in range(NCH + RAW, 2 * NCH):
                sp.wait_ge(wlo_done, j - RAW + 1)
                load_w(j)
            store_x1(TILES - 1, 1)
            sp.wait_ge(x1_stored[1], 16 * (TILES // 2))

            store_out(TILES, 0)

            def step1(T, s):
                sp.wait_ge(res_done[0], T)
                sp.wait_ge(res_done[1], T)
                load_x1(T + 1 - TILES, 1 - s)
                store_out(T - 1, 1)
                store_out(T, 0)

            loop_steps(sp, TILES + 1, TILES - 2, step1)
            store_out(LAST - 1, 1)
            store_out(LAST, 0)
            store_out(LAST, 1)
            for h in range(2):
                sp.wait_ge(out_stored[h], 16 * TILES)

        N_CONSTS = 8 + EXP

        @block.gpsimd
        def _(pool):
            pool.memset(ident[:, :], 0.0).then_inc(ident_zero, 1)
            pool.memset(ones[:, :], 1.0).then_inc(consts, 1)
            pool.wait_ge(ident_zero, 1)
            pool.affine_select(out=ident[:, :], in_=ident[:, :], compare_op=ALU.not_equal, fill=1.0, base=0,
                               pattern=[[-1, P]], channel_multiplier=1).then_inc(consts, 1)
            for k in range(EXP):
                pool.memset(inv_k[:, k:k + 1], 1.0 / (k + 1)).then_inc(consts, 1)
            pool.memset(keep[:, 0:1], 1.0).then_inc(consts, 1)
            pool.memset(u_sb[:, RANK:P], 0.0).then_inc(consts, 1)
            pool.wait_ge(consts, N_CONSTS - 4)
            pool.memset(hi(ut_hi[RANK:RANK + 1, :]), 1.0).then_inc(consts, 1)
            pool.wait_ge(consts, N_CONSTS - 3)
            pool.memset(hi(ut_lo[RANK:RANK + 1, :]), 0.0).then_inc(consts, 1)
            pool.wait_ge(consts, N_CONSTS - 2)
            pool.memset(hi(agg_hi[:, :, :, :]), 0.0).then_inc(consts, 1)
            pool.memset(hi(agg_lo[:, :, :, :]), 0.0).then_inc(consts, 1)

        @block.scalar
        def _(act):
            act.dma_start(pk[:, :], pack).then_inc(s_pk, 16)
            act.dma_start(rw[:, :], rows.partition_broadcast(P)).then_inc(s_rw, 16)
            for g in range(GROUPS):
                src = bass.AP(toep.tensor, g * GC * TOEP * GC, [[TOEP * GC, GC], [GC, POS], [1, 2 * P]])
                act.dma_start(mixed[:, 2 * g:2 * g + 2, :].rearrange("p a b -> p (a b)"), src).then_inc(s_toep, 16)
            act.dma_start(lb_raw[0:RANK + 1, :], bcat0).then_inc(s_lb, 16)
            act.dma_start(bk[:, :], bias_k).then_inc(s_bk, 16)
            for j in range(4):
                src = mixw[:, j * OQ * CH:(j + 1) * OQ * CH].rearrange("k (o i) -> k o i", i=CH)
                for n in range(2):
                    act.dma_start(mixw_at(j)[:, :, n, :], src).then_inc(s_mixw, 16)

            def split_src(T, loaded_sem, loaded, n, raw):
                act.wait_ge(loaded_sem, loaded)
                act.copy(src_hi[:, 0:n], raw).then_inc(srchi_done, 1)

            def split_w(j):
                cols = W0COLS if j < NCH else W1COLS
                act.wait_ge(w_loaded[j % RAW], 16 * (j // RAW + 1))
                if j >= NCH:
                    act.wait_ge(w_free, j - NCH + 1)
                act.copy(w_hi[:, j % NCH, 0:cols], w_raw[:, j % RAW, 0:cols]).then_inc(whi_done, 1)

            def gelu(m):
                act.wait_ge(mlp_mm, m + 1)
                act.activation(hg[:, m, :], hidp[:, NB * m:NB * m + NB], ACT.Gelu,
                               bias=pk[:, PK_B0 + m:PK_B0 + m + 1]).then_inc(mlp_h, 1)

            def split_act(T, s, per_bank, first=False):
                if not first:
                    act.wait_ge(half_done[1], T - 1)
                for b in range(2):
                    act.wait_ge(sum_done, 2 * T + (1 + b if per_bank else 2))
                    act.copy(act_hi[:, s, 4 * b:4 * b + 4, :], mixed[:, 4 * b:4 * b + 4, :]).then_inc(acthi_done, 1)

            def split_ut(T, rows_, first=False):
                act.wait_ge(ut_done, T + 1)
                if not first:
                    act.wait_ge(half_done[1], T)
                act.copy(ut_hi[0:rows_, :], utp[0:rows_, 0:P]).then_inc(uthi_done, 1)

            def gate_exp(T):
                act.wait_ge(gate_max, T + 1)
                act.activation(ex[:, :], sc[:, 0:4], ACT.Exp, bias=st[:, 0:1],
                               accum_out=st[:, 1:2]).then_inc(exp_done, 1)

            N0 = 2 * GROUPS * QX
            split_src(0, src_loaded, 16, N0, blk_raw[:, :])
            act.wait_ge(s_toep, 16 * GROUPS)
            act.copy(toep_hi[:, :, :], mixed[:, :, :].rearrange("p (g a) b -> p g (a b)", g=GROUPS)).then_inc(toephi_done, 1)
            gelu(0)
            split_w(0)
            gelu(1)
            split_w(1)
            split_act(0, 0, False, first=True)
            split_w(2)
            act.wait_ge(att_op, 3)
            act.activation(att[:, 1, :], att[:, 0, :], ACT.Exp, bias=stat[:, 1:2],
                           accum_out=stat[:, 2:3]).then_inc(att_exp, 1)
            for j in range(3, 6):
                split_w(j)
            act.wait_ge(src_loaded, 32)
            act.wait_ge(mix_done, 2)
            act.copy(src_hi[:, 0:N0], blk_raw[:, :]).then_inc(srchi_done, 1)
            for j in range(6, NCH):
                split_w(j)
            act.wait_ge(s_lb, 16)
            act.copy(lb_hi[0:RANK + 1, :], lb_raw[0:RANK + 1, :]).then_inc(lbhi_done, 1)

            act.wait_ge(consts, N_CONSTS)
            def split_agg(r):
                act.wait_ge(agg_mm, r + 1)
                for n in range(2):
                    p0 = CH * n
                    src = agg_ps[p0:p0 + CH, :, :].rearrange("p o (t n) -> p n t o", n=2)[:, n]
                    act.copy(agg_hi[p0:p0 + CH, :, n, 32 * r:32 * r + 32], src).then_inc(agghi_done, 1)

            def step0(T, s):
                gate_exp(T)
                split_ut(T, RANK)
                split_act(T + 1, 1 - s, False)

            def next_blocks(T):
                act.wait_ge(mix_done, 2 * T + 4)
                split_src(T + 2, src_loaded, 16 * T + 48, N0, blk_raw[:, :])

            split_agg(0)
            gate_exp(0)
            split_agg(1)
            split_ut(0, RANK, first=True)
            split_act(1, 1, False, first=True)
            for r in range(2):
                act.wait_ge(aggb_mm, r + 1)
                act.copy(aggb_row[:, 8 * r:8 * r + 8, :].rearrange("p t c -> p (t c)"),
                         acc[:, 1, :, :].rearrange("p h c -> p (h c)")).then_inc(aggb_done, 1)
            next_blocks(0)

            def body(T, s):
                step0(T, s)
                next_blocks(T)

            loop_steps(act, 1, TILES - 4, body)
            body(TILES - 3, 1)
            step0(TILES - 2, 0)
            act.wait_ge(mix_done, 2 * TILES)
            split_src(TILES, x1_loaded[0], 16, D, x1_slot(0))
            gate_exp(TILES - 1)
            split_ut(TILES - 1, RANK)
            split_act(TILES, 0, True)
            for j in range(NCH, 2 * NCH):
                split_w(j)
            act.wait_ge(s_lb, 32)
            act.wait_ge(half_done[1], TILES)
            act.copy(lb_hi[:, :], lb_raw[:, :]).then_inc(lbhi_done, 1)

            def step1(T, s, loaded):
                split_ut(T, P)
                act.wait_ge(mix_done, 2 * T + 2)
                split_src(T + 1, x1_loaded[1 - s], loaded, D, x1_slot(1 - s))
                split_act(T + 1, 1 - s, True)

            T = TILES
            act.wait_ge(mix_done, 2 * T + 2)
            split_src(T + 1, x1_loaded[1], 16, D, x1_slot(1))
            split_act(T + 1, 1, True)
            split_ut(T, P)
            with act.Fori(0, (TILES - 2) // 2) as i:
                step1(2 * i + (TILES + 1), 1, 16 * i + 32)
                step1(2 * i + (TILES + 2), 0, 16 * i + 32)
            split_ut(LAST, P)

        @block.vector
        def _(dve):
            def split_src(T, n, raw):
                dve.wait_ge(srchi_done, T + 1)
                dve.tensor_tensor(src_lo[:, 0:n], raw, hi(src_hi[:, 0:n]), ALU.subtract).then_inc(srclo_done, 1)

            def split_w(j):
                cols = W0COLS if j < NCH else W1COLS
                dve.wait_ge(whi_done, j + 1)
                dve.tensor_tensor(w_lo[:, j % NCH, 0:cols], w_raw[:, j % RAW, 0:cols],
                                  hi(w_hi[:, j % NCH, 0:cols]), ALU.subtract).then_inc(wlo_done, 1)

            def sum_conv(T, first=False):
                if not first:
                    dve.wait_ge(acthi_done, 2 * T)
                    dve.wait_ge(actlo_done, 2 * T)
                for n in range(2):
                    dve.wait_ge(mix_done, 2 * T + n + 1)
                    row = ctx_row[:, bass.ds(T, 1), CH * n:CH * n + CH].to_broadcast([P, POS, CH])
                    dve.tensor_tensor(mixed[:, :, CH * n:CH * n + CH],
                                      mixp[:, n, :].rearrange("p (a c) -> p a c", c=CH), row,
                                      ALU.add).then_inc(sum_done, 1)

            def sum_mix(T):
                dve.wait_ge(acthi_done, 2 * T)
                dve.wait_ge(actlo_done, 2 * T)
                for b in range(2):
                    dve.wait_ge(mix_done, 2 * T + b + 1)
                    row = aggb_row[:, bass.ds(T - TILES, 1), :].to_broadcast([P, 4, P])
                    dve.tensor_tensor(mixed[:, 4 * b:4 * b + 4, :],
                                      mixp[:, b, :].rearrange("p (a c) -> p a c", c=P), row,
                                      ALU.add).then_inc(sum_done, 1)

            def split_act(T, s):
                for b in range(2):
                    dve.wait_ge(acthi_done, 2 * T + b + 1)
                    dve.tensor_tensor(act_lo[:, s, 4 * b:4 * b + 4, :], mixed[:, 4 * b:4 * b + 4, :],
                                      hi(act_hi[:, s, 4 * b:4 * b + 4, :]), ALU.subtract).then_inc(actlo_done, 1)

            def split_ut(T, rows_):
                dve.wait_ge(uthi_done, T + 1)
                dve.tensor_tensor(ut_lo[0:rows_, :], utp[0:rows_, 0:P], hi(ut_hi[0:rows_, :]),
                                  ALU.subtract).then_inc(utlo_done, 1)

            def gate0(T, first=False):
                base = [0]

                def link(ins):
                    base[0] += 1
                    ins.then_inc(gate_op, 1)
                    dve.wait_ge(gate_op, GATE0 * T + base[0])

                dve.wait_ge(hid_done, T + 1)
                if not first:
                    dve.wait_ge(ut_done, T)
                link(dve.tensor_tensor(sc[:, 0:4], hidp[:, RANK:HID0], rw[:, RW_GB:RW_GB + 4], ALU.add))
                link(dve.tensor_tensor_scan(pm[:, 0:4], sc[:, 0:4], sc[:, 0:4], -3.4e38, ALU.max, ALU.max))
                dve.tensor_scalar(st[:, 0:1], pm[:, 3:4], -1.0, None, ALU.mult).then_inc(gate_max, 1)
                link(dve.tensor_scalar(keep[:, 1:4], pm[:, 0:3], pm[:, 3:4], None, ALU.is_lt))
                dve.wait_ge(exp_done, T + 1)
                link(dve.reciprocal(st[:, 2:3], st[:, 1:2]))
                link(dve.reciprocal(st[:, 3:4], st[:, 2:3]))
                link(dve.tensor_tensor(st[:, 4:5], st[:, 2:3], st[:, 3:4], ALU.mult))
                link(dve.tensor_scalar(kw[:, 0:4], keep[:, :], st[:, 4:5], None, ALU.mult))
                lo_ = 0
                for j, r in enumerate(RANKS):
                    ins = dve.tensor_scalar(u_sb[:, lo_:r], hidp[:, lo_:r], kw[:, j:j + 1], None, ALU.mult)
                    lo_ = r
                    if j < 2:
                        ins.then_inc(gate_op, 1)
                    elif j == 2:
                        ins.then_inc(gated, 1)
                    else:
                        ins.then_inc(gated, 1)

            def gate1(T):
                n0 = GATE0 * TILES + (T - TILES) * GATE1
                base = [0]

                def link(ins):
                    base[0] += 1
                    ins.then_inc(gate_op, 1)
                    dve.wait_ge(gate_op, n0 + base[0])

                dve.wait_ge(hid_done, T + 1)
                dve.wait_ge(ut_done, T)
                link(dve.tensor_tensor(gs[:, 0, :], hidp[:, P:HID1], rw[:, RW_RB:RW_RB + EXP], ALU.add))
                dve.nop(nofuse=True)
                link(dve.max(gs[:, 1, :], gs[:, 0, :]))
                link(dve.tensor_tensor_scan(gs[:, 2, :], ones[:, 0:EXP], gs[:, 1, :], -1.0, ALU.mult, ALU.add))
                link(dve.tensor_tensor(gs[:, 3, :], gs[:, 2, :], inv_k[:, :], ALU.mult))
                link(dve.tensor_reduce(st[:, 0:1], gs[:, 3, :], AX_X, ALU.max))
                link(dve.tensor_scalar(sc[:, :], gs[:, 0, :], st[:, 0:1], 0.0, ALU.subtract, ALU.max))
                dve.tensor_tensor(u_sb[:, :].rearrange("p (e r) -> p e r", r=ER),
                                  hidp[:, 0:P].rearrange("p (e r) -> p e r", r=ER),
                                  sc[:, :].unsqueeze(2).to_broadcast([P, EXP, ER]), ALU.mult).then_inc(gated, 2)

            def res0(T, s, h, loaded):
                cols = slice(h * HALF, (h + 1) * HALF)
                if h == 0:
                    dve.wait_ge(xs_loaded[s], loaded)
                dve.wait_ge(half_done[h], T + 1)
                dve.tensor_tensor(xs[s][:, cols], acc[:, s, h, :], xs[s][:, cols], ALU.add).then_inc(res_done[h], 1)

            def res1(T, s, h, first=False):
                cols = slice(h * HALF, (h + 1) * HALF)
                dve.wait_ge(half_done[h], T + 1)
                if first:
                    dve.wait_ge(x1_stored[1], 16 * (TILES // 2))
                else:
                    dve.wait_ge(out_stored[h], 16 * (T - TILES))
                dve.tensor_tensor(xs[1][:, cols], acc[:, s, h, :], bbase[:, cols], ALU.add).then_inc(biased, 1)
                dve.wait_ge(biased, 2 * (T - TILES) + h + 1)
                dve.tensor_tensor(xs[1][:, cols], xs[1][:, cols], x1_slot(s)[:, cols], ALU.add).then_inc(res_done[h], 1)

            dve.wait_ge(s_pk, 16)
            for r in range(4):
                a = pk[:, PK_C + 8 * r:PK_C + 8 * r + 8].unsqueeze(2).to_broadcast([P, 8, CH])
                b = pk[:, PK_CW:PK_CW + CH].unsqueeze(1).to_broadcast([P, 8, CH])
                dve.tensor_tensor(ctx_row[:, 4 * r:4 * r + 4, :].rearrange("p t (n c) -> p (t n) c", c=CH), a, b,
                                  ALU.mult).then_inc(ctx_prod, 1)

            N0 = 2 * GROUPS * QX
            split_src(0, N0, blk_raw[:, :])
            dve.wait_ge(toephi_done, 1)
            dve.tensor_tensor(toep_lo[:, :, :], mixed[:, :, :].rearrange("p (g a) b -> p g (a b)", g=GROUPS),
                              hi(toep_hi[:, :, :]), ALU.subtract).then_inc(toeplo_done, 1)
            split_w(0)
            dve.wait_ge(s_rw, 16)
            for r in range(4):
                dve.wait_ge(ctx_mm, r + 1)
                fs = rw[:, RW_FS:RW_FS + CH].unsqueeze(1).to_broadcast([P, 8, CH])
                dve.tensor_tensor(ctx_row[:, 4 * r:4 * r + 4, :].rearrange("p t (n c) -> p (t n) c", c=CH),
                                  acc[:, r // 2, r % 2, :].rearrange("p (n c) -> p n c", c=CH), fs,
                                  ALU.add).then_inc(ctx_ready, 1)
            dve.wait_ge(toeplo_done, 1)
            dve.wait_ge(ctx_ready, 4)
            sum_conv(0, first=True)
            split_w(1)
            split_act(0, 0)

            dve.wait_ge(mlp_mm, 3)
            dve.tensor_tensor(att[:, 0, :], hidp[0:NB, 2 * NB:2 * NB + KMIX], rw[0:NB, RW_B2:RW_B2 + KMIX],
                              ALU.add).then_inc(att_op, 1)
            dve.wait_ge(att_op, 1)
            dve.tensor_reduce(stat[:, 0:1], att[:, 0, :], AX_X, ALU.max).then_inc(att_op, 1)
            dve.wait_ge(att_op, 2)
            dve.tensor_scalar(stat[:, 1:2], stat[:, 0:1], -1.0, None, ALU.mult).then_inc(att_op, 1)
            split_w(2)
            dve.wait_ge(att_exp, 1)
            dve.reciprocal(stat[:, 3:4], stat[:, 2:3]).then_inc(att_op, 1)
            dve.wait_ge(att_op, 4)
            dve.tensor_scalar(att[:, 2, :], att[:, 1, :], stat[:, 3:4], None, ALU.mult).then_inc(att_op, 1)
            split_w(3)
            dve.wait_ge(att_t, 1)
            for j in range(4):
                dve.tensor_copy(attT[32 * j:32 * j + KMIX, :], utp[0:KMIX, 0:NB]).then_inc(att_copied, 1)
            dve.wait_ge(att_copied, 4)
            dve.wait_ge(s_bk, 16)
            dve.tensor_tensor(aggb_row[0:KMIX, :, :].rearrange("p t (n c) -> p (t n) c", c=CH),
                              attT[0:KMIX, :].unsqueeze(2).to_broadcast([KMIX, NB, CH]),
                              bk[:, :].unsqueeze(1).to_broadcast([KMIX, NB, CH]), ALU.mult).then_inc(aggb_prod, 1)
            for j in range(4, 6):
                split_w(j)
            split_src(1, N0, blk_raw[:, :])
            for j in range(6, NCH):
                split_w(j)
            dve.wait_ge(lbhi_done, 1)
            dve.tensor_tensor(lb_lo[0:RANK + 1, :], lb_raw[0:RANK + 1, :], hi(lb_hi[0:RANK + 1, :]),
                              ALU.subtract).then_inc(lblo_done, 1)
            dve.wait_ge(consts, N_CONSTS)

            def split_agg(r):
                for n in range(2):
                    dve.wait_ge(agghi_done, 2 * r + n + 1)
                    p0 = CH * n
                    src = agg_ps[p0:p0 + CH, :, :].rearrange("p o (t n) -> p n t o", n=2)[:, n]
                    dst = slice(32 * r, 32 * r + 32)
                    dve.tensor_tensor(agg_lo[p0:p0 + CH, :, n, dst], src, hi(agg_hi[p0:p0 + CH, :, n, dst]),
                                      ALU.subtract).then_inc(agglo_done, 1)

            split_agg(0)

            gate0(0, first=True)
            split_agg(1)
            split_ut(0, RANK)
            sum_conv(1)
            split_act(1, 1)
            split_src(2, N0, blk_raw[:, :])
            res0(0, 0, 0, 16)
            res0(0, 0, 1, 16)

            def step0(T, s, loaded):
                gate0(T)
                split_ut(T, RANK)
                res0(T, s, 0, loaded)
                sum_conv(T + 1)
                split_act(T + 1, 1 - s)
                split_src(T + 2, N0, blk_raw[:, :])
                res0(T, s, 1, loaded)

            with dve.Fori(0, (TILES - 4) // 2) as i:
                step0(2 * i + 1, 1, 16 * i + 16)
                step0(2 * i + 2, 0, 16 * i + 32)
            step0(TILES - 3, 1, 16 * ((TILES - 3) // 2 + 1))
            T = TILES - 2
            gate0(T)
            split_ut(T, RANK)
            res0(T, 0, 0, 16 * (T // 2 + 1))
            sum_conv(T + 1)
            split_act(T + 1, 1)
            split_src(TILES, D, x1_slot(0))
            res0(T, 0, 1, 16 * (T // 2 + 1))
            T = TILES - 1
            gate0(T)
            split_ut(T, RANK)
            sum_mix(TILES)
            split_act(TILES, 0)
            for j in range(NCH, 2 * NCH):
                split_w(j)
            res0(T, 1, 0, 16 * (T // 2 + 1))
            res0(T, 1, 1, 16 * (T // 2 + 1))
            dve.wait_ge(lbhi_done, 2)
            dve.tensor_tensor(lb_lo[:, :], lb_raw[:, :], hi(lb_hi[:, :]), ALU.subtract).then_inc(lblo_done, 1)

            dve.wait_ge(s_bbase, 16)
            T = TILES
            split_src(T + 1, D, x1_slot(1))
            sum_mix(T + 1)
            split_act(T + 1, 1)
            gate1(T)
            split_ut(T, P)
            res1(T, 0, 0, first=True)
            res1(T, 0, 1, first=True)

            def step1(T, s):
                gate1(T)
                split_ut(T, P)
                split_src(T + 1, D, x1_slot(1 - s))
                res1(T, s, 0)
                sum_mix(T + 1)
                split_act(T + 1, 1 - s)
                res1(T, s, 1)

            loop_steps(dve, TILES + 1, TILES - 2, step1)
            gate1(LAST)
            split_ut(LAST, P)
            res1(LAST, 1, 0)
            res1(LAST, 1, 1)

        @block.tensor
        def _(pe):
            def three(dst, l_hi, l_lo, r_hi, r_lo, start, stop):
                pe.matmul(dst, l_hi, r_hi, start=start, stop=False)
                pe.matmul(dst, l_hi, r_lo, start=False, stop=False)
                return pe.matmul(dst, l_lo, r_hi, start=False, stop=stop)

            def conv(T, first=False):
                pe.wait_ge(srclo_done, T + 1)
                if not first:
                    pe.wait_ge(sum_done, 2 * T)
                for n in range(2):
                    for g in range(GROUPS):
                        at = (n * GROUPS + g) * QX
                        dst = mixp[:, n, :].rearrange("p (a c) -> p a c", c=CH)[:, :, g * GC:(g + 1) * GC]
                        for side in range(2):
                            l = slice(at + side, at + side + QB)
                            r = slice((1 - side) * P, (2 - side) * P)
                            ins = three(dst, src_hi[:, l], src_lo[:, l],
                                        toep_hi[:, g, r].rearrange("p (a c) -> p a c", c=GC),
                                        toep_lo[:, g, r].rearrange("p (a c) -> p a c", c=GC),
                                        side == 0, side == 1)
                    ins.then_inc(mix_done, 1)

            def mix(T):
                pe.wait_ge(srclo_done, T + 1)
                pe.wait_ge(sum_done, 2 * T)
                t = bass.ds(T - TILES, 1)
                r_hi = agg_hi[:, t, :, :].rearrange("p t n o -> p (t n o)")
                r_lo = agg_lo[:, t, :, :].rearrange("p t n o -> p (t n o)")
                for b in range(2):
                    for c in range(4):
                        l = slice((4 * b + c) * P, (4 * b + c + 1) * P)
                        ins = three(mixp[:, b, c * P:(c + 1) * P], src_hi[:, l], src_lo[:, l], r_hi, r_lo, True, True)
                    ins.then_inc(mix_done, 1)

            def hid(T, s, k, width):
                if k % 4 == 0:
                    pe.wait_ge(actlo_done, 2 * T + 1 + k // 4)
                return three(hidp[:, 0:width], act_hi[:, s, k, :], act_lo[:, s, k, :],
                             w_hi[:, k, D:D + width], w_lo[:, k, D:D + width], k == 0, k == NCH - 1)

            def hid_all(T, s, width):
                pe.wait_ge(gated, 2 * T)
                for k in range(NCH):
                    ins = hid(T, s, k, width)
                ins.then_inc(hid_done, 1)

            def dense(s, h, k):
                cols = slice(h * HALF, (h + 1) * HALF)
                return three(acc[:, s, h, :], act_hi[:, s, k, :], act_lo[:, s, k, :],
                             w_hi[:, k, cols], w_lo[:, k, cols], k == 0, False)

            def acc_free(T, h):
                pe.wait_ge(res_done[h], T - 1)

            def turn_u(T, first=False):
                pe.wait_ge(gated, 2 * T + 2)
                if not first:
                    pe.wait_ge(utlo_done, T)
                pe.transpose(utp[:, 0:P], u_sb[:, :], ident[:, :]).then_inc(ut_done, 1)

            def lora_out(T, s, h, rows_):
                cols = slice(h * HALF, (h + 1) * HALF)
                pe.wait_ge(utlo_done, T + 1)
                three(acc[:, s, h, :], ut_hi[0:rows_, :], ut_lo[0:rows_, :], lb_hi[0:rows_, cols], lb_lo[0:rows_, cols],
                      False, True).then_inc(half_done[h], 1)

            def mlp(m, rhs):
                w = pk[:, PK_W0 + EMB * m:PK_W0 + EMB * (m + 1)]
                pe.matmul(hidp[:, NB * m:NB * m + NB], w, rhs, start=True, stop=True).then_inc(mlp_mm, 1)

            pe.wait_ge(s_pk, 16)
            mlp(0, pk[:, PK_C:PK_C + NB])
            pe.wait_ge(consts, 1)
            for r in range(4):
                pe.wait_ge(ctx_prod, r + 1)
                pe.matmul(acc[:, r // 2, r % 2, :], ones[:, :],
                          ctx_row[:, 4 * r:4 * r + 4, :].rearrange("p t c -> p (t c)"),
                          start=True, stop=True).then_inc(ctx_mm, 1)
            pe.wait_ge(mlp_h, 1)
            mlp(1, hg[:, 0, :])
            pe.wait_ge(toeplo_done, 1)
            conv(0, first=True)
            pe.wait_ge(mlp_h, 2)
            pe.matmul(hidp[0:NB, 2 * NB:2 * NB + KMIX], hg[:, 1, :], pk[:, PK_W2:PK_W2 + KMIX],
                      start=True, stop=True).then_inc(mlp_mm, 1)
            pe.wait_ge(consts, N_CONSTS)
            pe.wait_ge(att_op, 5)
            pe.transpose(utp[0:KMIX, 0:NB], att[:, 2, :], ident[0:NB, 0:NB]).then_inc(att_t, 1)

            def agg_round(r):
                for o in range(32):
                    j, oo = (32 * r + o) // OQ, (32 * r + o) % OQ
                    w = mixw_at(j)[:, oo].rearrange("k n i -> k (n i)")
                    ins = pe.matmul(agg_ps[:, o, :], w, attT[32 * j:32 * j + KMIX, :], start=True, stop=True)
                ins.then_inc(agg_mm, 1)

            def aggb_round(r):
                for h in range(2):
                    src = aggb_row[0:KMIX, 8 * r + 4 * h:8 * r + 4 * h + 4, :].rearrange("p t c -> p (t c)")
                    ins = pe.matmul(acc[:, 1, h, :], ones[0:KMIX, :], src, start=True, stop=True)
                ins.then_inc(aggb_mm, 1)

            def split_chunk(T, s, k, width, chunk):
                pe.wait_ge(wlo_done, chunk + 1)
                dense(s, 0, k)
                dense(s, 1, k)
                return hid(T, s, k, width)

            pe.wait_ge(ctx_ready, 4)
            pe.wait_ge(actlo_done, 1)
            pe.wait_ge(att_op, 1)
            for k in range(NCH):
                if k == 4:
                    pe.wait_ge(actlo_done, 2)
                ins = split_chunk(0, 0, k, HID0, k)
                if k == 0:
                    pe.wait_ge(att_copied, 4)
                    pe.wait_ge(s_mixw, 128)
                    agg_round(0)
                if k == NCH - 1:
                    ins.then_inc(hid_done, 1)
            conv(1)
            pe.wait_ge(agghi_done, 2)
            pe.wait_ge(agglo_done, 2)
            agg_round(1)
            turn_u(0, first=True)
            pe.wait_ge(agghi_done, 4)
            pe.wait_ge(agglo_done, 4)
            pe.wait_ge(aggb_prod, 1)
            aggb_round(0)
            pe.wait_ge(lblo_done, 1)
            lora_out(0, 0, 0, RANK + 1)
            lora_out(0, 0, 1, RANK + 1)
            pe.wait_ge(aggb_done, 1)
            aggb_round(1)

            def step0(T, s, acc_wait=True):
                hid_all(T, s, HID0)
                if acc_wait:
                    acc_free(T, 0)
                else:
                    pe.wait_ge(aggb_done, 2)
                for k in range(NCH):
                    dense(s, 0, k)
                    if k == NCH - 2:
                        turn_u(T)
                lora_out(T, s, 0, RANK + 1)
                conv(T + 1)
                if acc_wait:
                    acc_free(T, 1)
                for k in range(NCH):
                    dense(s, 1, k)
                lora_out(T, s, 1, RANK + 1)

            step0(1, 1, acc_wait=False)
            step0(2, 0)
            loop_steps(pe, 3, TILES - 4, step0)
            T = TILES - 1
            hid_all(T, 1, HID0)
            mix(TILES)
            acc_free(T, 0)
            acc_free(T, 1)
            for k in range(NCH):
                dense(1, 0, k)
                dense(1, 1, k).then_inc(w_free, 1)
                if k == 2:
                    turn_u(T)
            lora_out(T, 1, 0, RANK + 1)
            lora_out(T, 1, 1, RANK + 1)

            T = TILES
            pe.wait_ge(gated, 2 * T)
            acc_free(T, 0)
            acc_free(T, 1)
            pe.wait_ge(actlo_done, 2 * T + 2)
            for k in range(NCH):
                ins = split_chunk(T, 0, k, HID1, NCH + k)
            ins.then_inc(hid_done, 1)
            mix(T + 1)
            turn_u(T)
            pe.wait_ge(lblo_done, 2)
            lora_out(T, 0, 0, P)
            lora_out(T, 0, 1, P)

            def step1(T, s, last=False):
                hid_all(T, s, HID1)
                acc_free(T, 0)
                for k in range(NCH):
                    dense(s, 0, k)
                    if k == 4:
                        turn_u(T)
                lora_out(T, s, 0, P)
                acc_free(T, 1)
                for k in range(NCH):
                    dense(s, 1, k)
                    if k == 3 and not last:
                        mix(T + 1)
                lora_out(T, s, 1, P)

            loop_steps(pe, TILES + 1, TILES - 2, step1)
            step1(LAST, 1, last=True)


_OUT = (NB, CH, D)


def _layout(inp):
    a = {k: np.asarray(v) for k, v in inp.items()}
    x = a["x"]
    xp = np.pad(x, ((0, 0), (0, 0), (PAD, PAD))).reshape(TILES, 2, GROUPS, GC, QX, POS)[..., ::-1]
    xblk = xp.transpose(0, 3, 5, 1, 2, 4).reshape(TILES, P, 2 * GROUPS * QX)
    toep = np.zeros((GROUPS, GC, TOEP, GC), np.float32)
    w = a["L0_cond_weight"].reshape(GROUPS, GC, GC, TAPS)[..., ::-1]
    toep[:, :, POS - 1:POS - 1 + TAPS, :] = w.transpose(0, 2, 3, 1)
    wcat0 = np.concatenate([a["L0_ffn_W"], a["L0_ffn_A"], a["L0_ffn_gate_w"]]).T.reshape(P, NCH, W0COLS)
    lora_a = a["L1_ffn_lora_A"].transpose(0, 2, 1).reshape(EXP * ER, D)
    wcat1 = np.concatenate([a["L1_ffn_W_base"], lora_a, a["L1_ffn_W_router"]]).T
    wcat1 = wcat1.reshape(NCH, P, W1COLS).transpose(1, 0, 2)
    bcat0 = np.concatenate([a["L0_ffn_B"].T, a["L0_ffn_b"][None]])
    pack = np.concatenate([a["cond_128"].T, a["L0_cond_c_weight"].T, a["L1_cond_W0"], a["L1_cond_W1"],
                           a["L1_cond_W2"], a["L1_cond_b0"][:, None], a["L1_cond_b1"][:, None]], axis=1)
    rows = np.concatenate([a["fside_S_0"], a["L0_ffn_gate_b"], a["L1_cond_b2"], a["L1_ffn_b_router"]])
    return {"x": x, "xblk": xblk, "toep": toep, "wcat0": wcat0, "bcat0": bcat0, "wcat1": wcat1,
            "bcat1": a["L1_ffn_lora_B"].reshape(P, D), "b_base": a["L1_ffn_b_base"], "pack": pack, "rows": rows,
            "mixw": a["L1_cond_weight"].reshape(KMIX, CH * CH), "bias_k": a["L1_cond_bias_k"]}


def kernel(**inputs):
    import concourse.bacc as bacc
    from concourse.bass_utils import run_bass_kernel_spmd

    nc = bacc.Bacc("TRN2", target_bir_lowering=False, num_devices=1)
    arrays, aps = {}, {}
    for name, a in _layout(inputs).items():
        a = np.ascontiguousarray(a)
        arrays[f"in_{name}"] = a
        aps[name] = nc.dram_tensor(f"in_{name}", a.shape, mybir.dt.from_np(a.dtype), kind="ExternalInput").ap()
    out = nc.dram_tensor("out_dram", _OUT, F32, kind="ExternalOutput").ap()
    build(nc, out=out, **aps)
    return run_bass_kernel_spmd(nc, [arrays], core_ids=[0]).results[0]["out_dram"]
```

```python
from contextlib import ExitStack

import numpy as np

import concourse.bass as bass
from concourse import mybir

F32 = mybir.dt.float32
F32R = mybir.dt.float32r
ALU = mybir.AluOpType
ACT = mybir.ActivationFunctionType
AX_X = mybir.AxisListType.X

P = 128
NB, CH, D = 32, 64, 1024
TILES = NB * CH // P
NCH = D // P
BANK = 512
GROUPS, TAPS, PAD = 4, 9, 4
GC = CH // GROUPS
POS = P // GC
QB = D // POS
QX = QB + 1
TOEP = 2 * POS + POS - 1
RANK = 64
RANKS = (8, 16, 32, 64)
HID0 = RANK + len(RANKS)
EXP, ER = 8, 16
HID1 = EXP * ER + EXP
W0COLS, W1COLS = D + HID0, D + HID1
PART_A, PART_B, PART_C = range(3)
COLS0 = [(0, 364), (364, 728), (728, W0COLS)]
COLS1 = [(0, 388), (388, 776), (776, W1COLS)]
KMIX = 8
OQ = P // KMIX
EMB = 128
WARM = 8

PK_C = 0
PK_CW = PK_C + NB
PK_W0 = PK_CW + CH
PK_W1 = PK_W0 + EMB
PK_W2 = PK_W1 + EMB
PK_B0 = PK_W2 + KMIX
PACK = PK_B0 + 2
RW_FS = 0
RW_GB = RW_FS + CH
RW_B2 = RW_GB + len(RANKS)
RW_RB = RW_B2 + KMIX
ROW = RW_RB + EXP


def build(nc, x, xblk, toep, wcat0, bcat0, wcat1, bcat1, b_base, pack, rows, mixw, bias_k, out):
    x_t = x.rearrange("(t n) c h -> t (n c) h", n=2)
    out_t = out.rearrange("(t n) c h -> t (n c) h", n=2)
    x1_t = nc.dram_tensor("x1_scratch", (TILES, P, D), F32, kind="Internal").ap()
    ctx_d = nc.dram_tensor("ctx_scratch", (NB, CH), F32, kind="Internal").ap()
    aggb_d = nc.dram_tensor("aggb_scratch", (NB, CH), F32, kind="Internal").ap()

    with ExitStack() as ctx:
        def sb(name, shape, dt=F32):
            return ctx.enter_context(nc.sbuf_tensor(name, shape, dt))

        def psum(name, shape):
            return ctx.enter_context(nc.psum_tensor(name, shape, F32))

        def sem(name):
            return ctx.enter_context(nc.semaphore(name))

        w_hi = sb("w_hi", [P, NCH, W1COLS], F32R)
        w_lo = sb("w_lo", [P, NCH, W1COLS], F32R)
        w_raw = sb("w_raw", [P, NCH, W1COLS])
        lb_hi = sb("lb_hi", [P, D], F32R)
        lb_lo = sb("lb_lo", [P, D], F32R)
        lb_raw = sb("lb_raw", [P, D])
        filt = sb("filt", [P, GROUPS, 2 * P])
        agg = sb("agg", [P, TILES, 2, CH])
        ctx_row = sb("ctx_row", [P, TILES, P])
        aggb_row = sb("aggb_row", [P, TILES, P])
        bbase = sb("bbase", [P, D])
        xs = [sb("xs0", [P, D]), sb("xs1", [P, D])]
        blk = [sb("blk0", [P, 2 * GROUPS * QX]), sb("blk1", [P, 2 * GROUPS * QX])]
        mixed = sb("mixed", [P, NCH, P])
        act_hi = sb("act_hi", [P, 2, NCH, P], F32R)
        act_lo = sb("act_lo", [P, 2, NCH, P], F32R)
        u_sb = sb("u_sb", [P, P])
        ut_hi = sb("ut_hi", [P, P], F32R)
        ut_lo = sb("ut_lo", [P, P], F32R)
        pk = sb("pk", [P, PACK])
        rw = sb("rw", [P, ROW])
        bk = sb("bk", [KMIX, CH])
        mixw_sb = sb("mixw_sb", [P, CH // OQ, 2, CH])
        diag = sb("diag", [P, OQ])
        ident = sb("ident", [P, P])
        ones = sb("ones", [P, P])
        inv_k = sb("inv_k", [P, EXP])
        hg = sb("hg", [P, 2, NB])
        ctx_sb = sb("ctx_sb", [NB, CH])
        aggb_sb = sb("aggb_sb", [NB, CH])
        att = sb("att", [NB, 3, KMIX])
        att_rep = sb("att_rep", [NB, OQ, KMIX])
        stat = sb("stat", [NB, 4])
        att_all = sb("att_all", [P, NB])
        att_diag = sb("att_diag", [P, OQ, NB])
        sc = sb("sc", [P, 8])
        pm = sb("pm", [P, 8])
        keep = sb("keep", [P, 4])
        kw = sb("kw", [P, 8])
        ex = sb("ex", [P, 4])
        st = sb("st", [P, 8])
        gs = sb("gs", [P, 4, EXP])

        acc_a = psum("acc_a", [P, 2, BANK])
        acc_b = psum("acc_b", [P, BANK])
        acc_c = psum("acc_c", [P, 2, BANK])
        mixp = psum("mixp", [P, 2, BANK])
        utp = psum("utp", [P, BANK])

        s_pk = sem("s_pk")
        s_rw = sem("s_rw")
        s_bk = sem("s_bk")
        s_mixw = sem("s_mixw")
        s_bbase = sem("s_bbase")
        s_filt = [sem(f"s_filt{g}") for g in range(GROUPS)]
        s_lb = sem("s_lb")
        ctx_first = sem("ctx_first")
        ctx_rest = sem("ctx_rest")
        aggb_loaded = sem("aggb_loaded")
        w_loaded = [sem(f"w_loaded{k}") for k in range(NCH)]
        blk_loaded = [sem("blk_loaded0"), sem("blk_loaded1")]
        xs_loaded = [sem("xs_loaded0"), sem("xs_loaded1")]
        ctx_stored = sem("ctx_stored")
        aggb_stored = sem("aggb_stored")
        xs_stored = [sem("xs_stored0"), sem("xs_stored1")]
        whi_done = sem("whi_done")
        wlo_done = sem("wlo_done")
        lbhi_done = sem("lbhi_done")
        lblo_done = sem("lblo_done")
        acthi_done = sem("acthi_done")
        actlo_done = sem("actlo_done")
        uthi_done = sem("uthi_done")
        utlo_done = sem("utlo_done")
        mix_done = sem("mix_done")
        sum_done = sem("sum_done")
        hid_done = sem("hid_done")
        gate_op = sem("gate_op")
        gate_max = sem("gate_max")
        exp_done = sem("exp_done")
        gated = sem("gated")
        ut_done = sem("ut_done")
        part_done = [sem("part_a_done"), sem("part_b_done"), sem("part_c_done")]
        biased = sem("biased")
        res_done = [sem("res_a_done"), sem("res_b_done"), sem("res_c_done")]
        w_free = sem("w_free")
        consts = sem("consts")
        ctx_mm = sem("ctx_mm")
        ctx_sum = sem("ctx_sum")
        mlp_mm = sem("mlp_mm")
        mlp_h = sem("mlp_h")
        att_op = sem("att_op")
        att_exp = sem("att_exp")
        att_t = sem("att_t")
        att_copied = sem("att_copied")
        att_diag_done = sem("att_diag_done")
        agg_mm = sem("agg_mm")
        agg_read = sem("agg_read")
        aggb_mm = sem("aggb_mm")
        aggb_copied = sem("aggb_copied")

        block = ctx.enter_context(nc.Block())
        LAST = 2 * TILES - 1
        GATE0, GATE1 = 7, 6
        N_CONSTS = 10 + EXP

        def hi(part):
            return part.bitcast(F32)

        def acc(c, s):
            return (acc_a[:, s, :], acc_b[:, :], acc_c[:, s, :])[c]

        def dense_cols(cols, c):
            return cols[c][0], min(cols[c][1], D)

        def loop_steps(eng, first, count, body):
            with eng.Fori(0, count // 2) as i:
                body(2 * i + first, first % 2, i + first // 2)
                body(2 * i + (first + 1), (first + 1) % 2, i + (first + 1) // 2)

        @block.sync
        def _(sp):
            def rows_of(dram, t):
                return dram[bass.ds(t, 1)].rearrange("a p h -> (a p) h")

            def load_blocks(t, s):
                sp.dma_start(blk[s][:, :], rows_of(xblk, t)).then_inc(blk_loaded[s], 16)

            def load_w(k, layer):
                wcat, cols = ((wcat0, W0COLS), (wcat1, W1COLS))[layer]
                sp.dma_start(w_raw[:, k, 0:cols], wcat[:, k, :]).then_inc(w_loaded[k], 16)

            def load_x(t, s):
                sp.dma_start(xs[s][:, :], rows_of(x_t, t)).then_inc(xs_loaded[s], 16)

            def load_x1(t, s):
                sp.dma_start(blk[s][:, 0:D], rows_of(x1_t, t)).then_inc(blk_loaded[s], 16)

            def store(dram, t, T, s):
                for c in range(3):
                    sp.wait_ge(res_done[c], T + 1)
                sp.dma_start(rows_of(dram, t), xs[s][:, :]).then_inc(xs_stored[s], 16)

            load_blocks(0, 0)
            for g in range(GROUPS):
                src = bass.AP(toep.tensor, g * GC * TOEP * GC, [[TOEP * GC, GC], [GC, POS], [1, 2 * P]])
                sp.dma_start(filt[:, g, :], src).then_inc(s_filt[g], 16)
            load_w(0, 0)
            load_w(1, 0)
            sp.wait_ge(ctx_sum, 1)
            sp.dma_start(ctx_d, ctx_sb[:, :]).then_inc(ctx_stored, 16)
            load_w(2, 0)
            sp.wait_ge(ctx_stored, 16)
            ctx_rows = ctx_d.rearrange("(t n) c -> t (n c)", n=2)
            sp.dma_start(ctx_row[:, 0, :], ctx_rows[0].partition_broadcast(P)).then_inc(ctx_first, 16)
            for k in range(3, NCH):
                load_w(k, 0)
            sp.dma_start(lb_raw[0:RANK + 1, :], bcat0).then_inc(s_lb, 16)
            load_blocks(1, 1)
            load_x(0, 0)
            sp.dma_start(ctx_row[:, 1:TILES, :].rearrange("p t c -> p (t c)"),
                         ctx_rows[1:TILES].rearrange("t c -> (t c)").partition_broadcast(P)).then_inc(ctx_rest, 16)
            sp.wait_ge(mix_done, 2)
            load_blocks(2, 0)
            load_x(1, 1)
            for k in range(NCH):
                sp.wait_ge(wlo_done, k + 1)
                load_w(k, 1)
            sp.wait_ge(lblo_done, 1)
            sp.dma_start(lb_raw[:, :], bcat1).then_inc(s_lb, 16)
            sp.wait_ge(aggb_copied, 1)
            sp.dma_start(aggb_d, aggb_sb[:, :]).then_inc(aggb_stored, 16)
            sp.wait_ge(aggb_stored, 16)
            sp.dma_start(aggb_row[:, :, :].rearrange("p t c -> p (t c)"),
                         aggb_d.rearrange("b c -> (b c)").partition_broadcast(P)).then_inc(aggb_loaded, 16)
            sp.dma_start(bbase[:, :], b_base.partition_broadcast(P)).then_inc(s_bbase, 16)

            def step0(T, s, pair):
                sp.wait_ge(mix_done, 2 * T + 2)
                load_blocks(T + 2, s)
                store(x1_t, T - 1, T - 1, 1 - s)
                sp.wait_ge(xs_stored[1 - s], 16 * pair + 16 * s)
                load_x(T + 1, 1 - s)

            loop_steps(sp, 1, TILES - 4, step0)
            step0(TILES - 3, 1, (TILES - 3) // 2)
            T = TILES - 2
            sp.wait_ge(mix_done, 2 * T + 2)
            load_x1(0, 0)
            store(x1_t, T - 1, T - 1, 1)
            sp.wait_ge(xs_stored[1], 16 * (T // 2))
            load_x(T + 1, 1)
            T = TILES - 1
            sp.wait_ge(mix_done, 2 * T + 2)
            load_x1(1, 1)
            store(x1_t, T - 1, T - 1, 0)
            store(x1_t, T, T, 1)
            for s in range(2):
                sp.wait_ge(xs_stored[s], 16 * (TILES // 2))

            def step1(T, s, pair):
                for c in range(3):
                    sp.wait_ge(res_done[c], T)
                load_x1(T + 1 - TILES, 1 - s)
                store(out_t, T - 1 - TILES, T - 1, 1 - s)

            loop_steps(sp, TILES + 1, TILES - 2, step1)
            store(out_t, TILES - 2, LAST - 1, 0)
            for c in (PART_C, PART_A, PART_B):
                a, b = dense_cols(COLS1, c)
                sp.wait_ge(res_done[c], LAST + 1)
                sp.dma_start(out_t[TILES - 1, :, a:b], xs[1][:, a:b]).then_inc(xs_stored[1], 16)
            sp.wait_ge(xs_stored[0], 16 * TILES)
            sp.wait_ge(xs_stored[1], 16 * (TILES + 2))

        @block.gpsimd
        def _(pool):
            pool.memset(ones[:, :], 1.0).then_inc(consts, 1)
            pool.memset(ident[:, :], 0.0).then_inc(consts, 1)
            pool.dma_start(rw[:, :], rows.partition_broadcast(P)).then_inc(s_rw, 16)
            pool.wait_ge(consts, 2)
            pool.affine_select(out=ident[:, :], in_=ident[:, :], compare_op=ALU.not_equal, fill=1.0, base=0,
                               pattern=[[-1, P]], channel_multiplier=1).then_inc(consts, 1)
            pool.affine_select(out=diag[:, :], in_=ones[:, 0:OQ], compare_op=ALU.is_ge, fill=0.0, base=0,
                               pattern=[[-KMIX, OQ]], channel_multiplier=1).then_inc(consts, 1)
            pool.wait_ge(consts, 4)
            pool.affine_select(out=diag[:, :], in_=diag[:, :], compare_op=ALU.is_ge, fill=0.0, base=KMIX - 1,
                               pattern=[[KMIX, OQ]], channel_multiplier=-1).then_inc(consts, 1)
            pool.dma_start(bk[:, :], bias_k).then_inc(s_bk, 16)
            for n in range(2):
                pool.dma_start(mixw_sb[:, :, n, :], mixw.rearrange("p (m i) -> p m i", i=CH)).then_inc(s_mixw, 16)
            for k in range(EXP):
                pool.memset(inv_k[:, k:k + 1], 1.0 / (k + 1)).then_inc(consts, 1)
            pool.memset(keep[:, 0:1], 1.0).then_inc(consts, 1)
            pool.memset(u_sb[:, RANK:P], 0.0).then_inc(consts, 1)
            pool.wait_ge(consts, N_CONSTS - 3)
            pool.memset(hi(ut_hi[RANK:RANK + 1, :]), 1.0).then_inc(consts, 1)
            pool.wait_ge(consts, N_CONSTS - 2)
            pool.memset(hi(ut_lo[RANK:RANK + 1, :]), 0.0).then_inc(consts, 1)
            pool.wait_ge(consts, N_CONSTS - 1)
            pool.memset(agg[:, :, :, :], 0.0).then_inc(consts, 1)

        @block.scalar
        def _(act):
            act.dma_start(pk[:, :], pack).then_inc(s_pk, 16)

            def split_w(k, layer):
                cols = (W0COLS, W1COLS)[layer]
                act.wait_ge(w_loaded[k], 16 * layer + 16)
                if layer:
                    act.wait_ge(w_free, k + 1)
                act.copy(w_hi[:, k, 0:cols], w_raw[:, k, 0:cols]).then_inc(whi_done, 1)

            def gelu(m):
                act.wait_ge(mlp_mm, m + 1)
                act.activation(hg[:, m, :], utp[:, NB * m:NB * m + NB], ACT.Gelu,
                               bias=pk[:, PK_B0 + m:PK_B0 + m + 1]).then_inc(mlp_h, 1)

            def split_act(T, s, per_bank, first=False):
                if not first:
                    act.wait_ge(part_done[PART_B], T - 1)
                for b in range(2):
                    act.wait_ge(sum_done, 2 * T + (1 + b if per_bank else 2))
                    act.copy(act_hi[:, s, 4 * b:4 * b + 4, :], mixed[:, 4 * b:4 * b + 4, :]).then_inc(acthi_done, 1)

            def split_ut(T, rows_, first=False):
                act.wait_ge(ut_done, T + 1)
                if not first:
                    act.wait_ge(part_done[PART_B], T)
                act.copy(ut_hi[0:rows_, :], utp[0:rows_, 0:P]).then_inc(uthi_done, 1)

            def gate_exp(T):
                act.wait_ge(gate_max, T + 1)
                act.activation(ex[:, :], sc[:, 0:4], ACT.Exp, bias=st[:, 0:1],
                               accum_out=st[:, 1:2]).then_inc(exp_done, 1)

            gelu(0)
            gelu(1)
            act.wait_ge(att_op, 3)
            act.activation(att[:, 1, :], att[:, 0, :], ACT.Exp, bias=stat[:, 1:2],
                           accum_out=stat[:, 2:3]).then_inc(att_exp, 1)
            split_w(0, 0)
            split_act(0, 0, False, first=True)
            for k in range(1, 6):
                split_w(k, 0)
            act.wait_ge(consts, N_CONSTS)

            def place_kernels(m):
                act.wait_ge(agg_mm, m + 1)
                src = (acc_a if m % 2 else acc_c)[:, 1, :].rearrange("p (o t n) -> p n t o", o=OQ, n=2)
                for n in range(2):
                    rows_ = slice(CH * n, CH * n + CH)
                    act.copy(agg[rows_, :, n, OQ * m:OQ * m + OQ], src[rows_, n]).then_inc(agg_read, 1)

            place_kernels(0)
            for k in range(6, NCH):
                split_w(k, 0)
            act.wait_ge(s_lb, 16)
            act.copy(lb_hi[0:RANK + 1, :], lb_raw[0:RANK + 1, :]).then_inc(lbhi_done, 1)
            place_kernels(1)

            gate_exp(0)
            place_kernels(2)
            split_ut(0, RANK, first=True)
            split_act(1, 1, False, first=True)
            place_kernels(3)

            def step0(T, s, pair):
                gate_exp(T)
                split_ut(T, RANK)
                split_act(T + 1, 1 - s, False)

            loop_steps(act, 1, TILES - 2, step0)
            T = TILES - 1
            gate_exp(T)
            split_ut(T, RANK)
            split_act(TILES, 0, True)
            for k in range(NCH):
                split_w(k, 1)
            act.wait_ge(s_lb, 32)
            act.wait_ge(part_done[PART_B], TILES)
            act.copy(lb_hi[:, :], lb_raw[:, :]).then_inc(lbhi_done, 1)

            T = TILES
            split_ut(T, P)
            split_act(T + 1, 1, True)

            def step1(T, s, pair):
                split_ut(T, P)
                split_act(T + 1, 1 - s, True)

            loop_steps(act, TILES + 1, TILES - 2, step1)
            split_ut(LAST, P)

        @block.vector
        def _(dve):
            def split_w(k, layer):
                cols = (W0COLS, W1COLS)[layer]
                dve.wait_ge(whi_done, NCH * layer + k + 1)
                dve.tensor_tensor(w_lo[:, k, 0:cols], w_raw[:, k, 0:cols],
                                  hi(w_hi[:, k, 0:cols]), ALU.subtract).then_inc(wlo_done, 1)

            def sum_conv(T, first=False):
                if not first:
                    dve.wait_ge(acthi_done, 2 * T)
                    dve.wait_ge(actlo_done, 2 * T)
                for n in range(2):
                    dve.wait_ge(mix_done, 2 * T + n + 1)
                    row = ctx_row[:, bass.ds(T, 1), CH * n:CH * n + CH].to_broadcast([P, POS, CH])
                    dve.tensor_tensor(mixed[:, :, CH * n:CH * n + CH],
                                      mixp[:, n, :].rearrange("p (a c) -> p a c", c=CH), row,
                                      ALU.add).then_inc(sum_done, 1)

            def sum_mix(T):
                dve.wait_ge(acthi_done, 2 * T)
                dve.wait_ge(actlo_done, 2 * T)
                for b in range(2):
                    dve.wait_ge(mix_done, 2 * T + b + 1)
                    row = aggb_row[:, bass.ds(T - TILES, 1), :].to_broadcast([P, 4, P])
                    dve.tensor_tensor(mixed[:, 4 * b:4 * b + 4, :],
                                      mixp[:, b, :].rearrange("p (a c) -> p a c", c=P), row,
                                      ALU.add).then_inc(sum_done, 1)

            def split_act(T, s):
                for b in range(2):
                    dve.wait_ge(acthi_done, 2 * T + b + 1)
                    dve.tensor_tensor(act_lo[:, s, 4 * b:4 * b + 4, :], mixed[:, 4 * b:4 * b + 4, :],
                                      hi(act_hi[:, s, 4 * b:4 * b + 4, :]), ALU.subtract).then_inc(actlo_done, 1)

            def split_ut(T, rows_):
                dve.wait_ge(uthi_done, T + 1)
                dve.tensor_tensor(ut_lo[0:rows_, :], utp[0:rows_, 0:P], hi(ut_hi[0:rows_, :]),
                                  ALU.subtract).then_inc(utlo_done, 1)

            def gate0(T, s, first=False):
                links = [0]

                def link(ins):
                    links[0] += 1
                    ins.then_inc(gate_op, 1)
                    dve.wait_ge(gate_op, GATE0 * T + links[0])

                hid = acc_c[:, s, D - COLS0[PART_C][0]:]
                dve.wait_ge(hid_done, T + 1)
                if not first:
                    dve.wait_ge(ut_done, T)
                link(dve.tensor_tensor(sc[:, 0:4], hid[:, RANK:HID0], rw[:, RW_GB:RW_GB + 4], ALU.add))
                link(dve.tensor_tensor_scan(pm[:, 0:4], sc[:, 0:4], sc[:, 0:4], -3.4e38, ALU.max, ALU.max))
                dve.tensor_scalar(st[:, 0:1], pm[:, 3:4], -1.0, None, ALU.mult).then_inc(gate_max, 1)
                link(dve.tensor_scalar(keep[:, 1:4], pm[:, 0:3], pm[:, 3:4], None, ALU.is_lt))
                dve.wait_ge(exp_done, T + 1)
                link(dve.reciprocal(st[:, 2:3], st[:, 1:2]))
                link(dve.reciprocal(st[:, 3:4], st[:, 2:3]))
                link(dve.tensor_tensor(st[:, 4:5], st[:, 2:3], st[:, 3:4], ALU.mult))
                link(dve.tensor_scalar(kw[:, 0:4], keep[:, :], st[:, 4:5], None, ALU.mult))
                r0 = 0
                for j, r in enumerate(RANKS):
                    dve.tensor_scalar(u_sb[:, r0:r], hid[:, r0:r], kw[:, j:j + 1], None, ALU.mult).then_inc(gated, 1)
                    r0 = r

            def gate1(T, s):
                n0 = GATE0 * TILES + (T - TILES) * GATE1
                links = [0]

                def link(ins):
                    links[0] += 1
                    ins.then_inc(gate_op, 1)
                    dve.wait_ge(gate_op, n0 + links[0])

                hid = acc_c[:, s, D - COLS1[PART_C][0]:]
                dve.wait_ge(hid_done, T + 1)
                dve.wait_ge(ut_done, T)
                link(dve.tensor_tensor(gs[:, 0, :], hid[:, P:HID1], rw[:, RW_RB:RW_RB + EXP], ALU.add))
                dve.nop(nofuse=True)
                link(dve.max(gs[:, 1, :], gs[:, 0, :]))
                link(dve.tensor_tensor_scan(gs[:, 2, :], ones[:, 0:EXP], gs[:, 1, :], -1.0, ALU.mult, ALU.add))
                link(dve.tensor_tensor(gs[:, 3, :], gs[:, 2, :], inv_k[:, :], ALU.mult))
                link(dve.tensor_reduce(st[:, 0:1], gs[:, 3, :], AX_X, ALU.max))
                link(dve.tensor_scalar(sc[:, :], gs[:, 0, :], st[:, 0:1], 0.0, ALU.subtract, ALU.max))
                dve.tensor_tensor(u_sb[:, :].rearrange("p (e r) -> p e r", r=ER),
                                  hid[:, 0:P].rearrange("p (e r) -> p e r", r=ER),
                                  sc[:, :].unsqueeze(2).to_broadcast([P, EXP, ER]), ALU.mult).then_inc(gated, 4)

            def res0(T, s, pair, c):
                a, b = dense_cols(COLS0, c)
                dve.wait_ge(xs_loaded[s], 16 * pair + 16)
                dve.wait_ge(part_done[c], T + 1)
                dve.tensor_tensor(xs[s][:, a:b], acc(c, s)[:, 0:b - a], xs[s][:, a:b], ALU.add).then_inc(res_done[c], 1)

            def res1(T, s, pair, c):
                a, b = dense_cols(COLS1, c)
                dve.wait_ge(part_done[c], T + 1)
                dve.wait_ge(xs_stored[s], 16 * pair)
                dve.tensor_tensor(xs[s][:, a:b], acc(c, s)[:, 0:b - a], bbase[:, a:b], ALU.add).then_inc(biased, 1)
                order = (PART_C, PART_A, PART_B).index(c)
                dve.wait_ge(biased, 3 * (T - TILES) + order + 1)
                dve.tensor_tensor(xs[s][:, a:b], xs[s][:, a:b], blk[s][:, a:b], ALU.add).then_inc(res_done[c], 1)

            dve.wait_ge(ctx_mm, 1)
            dve.wait_ge(s_rw, 16)
            dve.tensor_tensor(ctx_sb[:, :], acc_b[0:NB, 0:CH], rw[0:NB, RW_FS:RW_FS + CH], ALU.add).then_inc(ctx_sum, 1)

            dve.wait_ge(mlp_mm, 3)
            dve.tensor_tensor(att[:, 0, :], utp[0:NB, 2 * NB:2 * NB + KMIX], rw[0:NB, RW_B2:RW_B2 + KMIX],
                              ALU.add).then_inc(att_op, 1)
            dve.wait_ge(att_op, 1)
            dve.tensor_reduce(stat[:, 0:1], att[:, 0, :], AX_X, ALU.max).then_inc(att_op, 1)
            dve.wait_ge(att_op, 2)
            dve.tensor_scalar(stat[:, 1:2], stat[:, 0:1], -1.0, None, ALU.mult).then_inc(att_op, 1)
            dve.wait_ge(att_exp, 1)
            dve.reciprocal(stat[:, 3:4], stat[:, 2:3]).then_inc(att_op, 1)
            dve.wait_ge(att_op, 4)
            dve.tensor_scalar(att_rep[:, :, :], att[:, 1, :].unsqueeze(1).to_broadcast([NB, OQ, KMIX]),
                              stat[:, 3:4], None, ALU.mult).then_inc(att_op, 1)
            dve.wait_ge(ctx_first, 16)
            split_w(0, 0)
            sum_conv(0, first=True)
            dve.wait_ge(att_t, 1)
            dve.tensor_copy(att_all[:, :], utp[:, 2 * P:2 * P + NB]).then_inc(att_copied, 1)
            split_act(0, 0)
            dve.wait_ge(att_copied, 1)
            dve.wait_ge(consts, 5)
            dve.tensor_tensor(att_diag[:, :, :], diag[:, :].unsqueeze(2).to_broadcast([P, OQ, NB]),
                              att_all[:, :].unsqueeze(1).to_broadcast([P, OQ, NB]), ALU.mult).then_inc(att_diag_done, 1)
            split_w(1, 0)
            split_w(2, 0)
            dve.wait_ge(aggb_mm, 1)
            dve.tensor_copy(aggb_sb[:, :], utp[0:NB, 3 * P:3 * P + CH]).then_inc(aggb_copied, 1)
            for k in range(3, NCH):
                split_w(k, 0)
            dve.wait_ge(lbhi_done, 1)
            dve.tensor_tensor(lb_lo[0:RANK + 1, :], lb_raw[0:RANK + 1, :], hi(lb_hi[0:RANK + 1, :]),
                              ALU.subtract).then_inc(lblo_done, 1)

            dve.wait_ge(consts, N_CONSTS)
            gate0(0, 0, first=True)
            split_ut(0, RANK)
            dve.wait_ge(ctx_rest, 16)
            sum_conv(1)
            split_act(1, 1)
            for c in (PART_C, PART_A, PART_B):
                res0(0, 0, 0, c)

            def step0(T, s, pair):
                gate0(T, s)
                split_ut(T, RANK)
                sum_conv(T + 1)
                split_act(T + 1, 1 - s)
                for c in (PART_C, PART_A, PART_B):
                    res0(T, s, pair, c)

            loop_steps(dve, 1, TILES - 2, step0)
            T = TILES - 1
            gate0(T, 1)
            dve.wait_ge(aggb_loaded, 16)
            sum_mix(TILES)
            split_act(TILES, 0)
            split_w(0, 1)
            split_ut(T, RANK)
            for k in range(1, 4):
                split_w(k, 1)
            res0(T, 1, T // 2, PART_B)
            split_w(4, 1)
            res0(T, 1, T // 2, PART_C)
            res0(T, 1, T // 2, PART_A)
            for k in range(5, NCH):
                split_w(k, 1)
            dve.wait_ge(lbhi_done, 2)
            dve.tensor_tensor(lb_lo[:, :], lb_raw[:, :], hi(lb_hi[:, :]), ALU.subtract).then_inc(lblo_done, 1)

            dve.wait_ge(s_bbase, 16)
            T = TILES
            gate1(T, 0)
            split_ut(T, P)
            sum_mix(T + 1)
            split_act(T + 1, 1)
            for c in (PART_C, PART_A, PART_B):
                res1(T, 0, T // 2, c)

            def step1(T, s, pair):
                gate1(T, s)
                split_ut(T, P)
                sum_mix(T + 1)
                split_act(T + 1, 1 - s)
                for c in (PART_C, PART_A, PART_B):
                    res1(T, s, pair, c)

            loop_steps(dve, TILES + 1, TILES - 2, step1)
            gate1(LAST, 1)
            split_ut(LAST, P)
            for c in (PART_C, PART_A, PART_B):
                res1(LAST, 1, LAST // 2, c)

        @block.tensor
        def _(pe):
            def three(dst, l_hi, l_lo, r_hi, r_lo, start, stop, skip=False):
                pe.matmul(dst, l_hi, r_hi, start=start, stop=False, skip_group_check=skip)
                pe.matmul(dst, l_hi, r_lo, start=False, stop=False, skip_group_check=skip)
                return pe.matmul(dst, l_lo, r_hi, start=False, stop=stop, skip_group_check=skip)

            def conv(T, s, pair, first=False):
                pe.wait_ge(blk_loaded[s], 16 * pair + 16)
                if not first:
                    pe.wait_ge(sum_done, 2 * T)
                for n in range(2):
                    for g in range(GROUPS):
                        if first and n == 0:
                            pe.wait_ge(s_filt[g], 16)
                        at = (n * GROUPS + g) * QX
                        dst = mixp[:, n, :].rearrange("p (a c) -> p a c", c=CH)[:, :, g * GC:(g + 1) * GC]
                        for side in range(2):
                            taps = filt[:, g, (1 - side) * P:(2 - side) * P].rearrange("p (a c) -> p a c", c=GC)
                            ins = pe.matmul(dst, blk[s][:, at + side:at + side + QB], taps,
                                            start=(side == 0), stop=(side == 1))
                    ins.then_inc(mix_done, 1)

            def mix(T, s, pair):
                pe.wait_ge(blk_loaded[s], 16 * pair + 16)
                pe.wait_ge(sum_done, 2 * T)
                mat = agg[:, bass.ds(T - TILES, 1), :, :].rearrange("p t n o -> p (t n o)")
                for b in range(2):
                    for c in range(4):
                        k = 4 * b + c
                        ins = pe.matmul(mixp[:, b, c * P:(c + 1) * P], blk[s][:, k * P:(k + 1) * P], mat,
                                        start=True, stop=True)
                    ins.then_inc(mix_done, 1)

            def dense(s, cols, c, k):
                a, b = cols[c]
                return three(acc(c, s)[:, 0:b - a], act_hi[:, s, k, :], act_lo[:, s, k, :],
                             w_hi[:, k, a:b], w_lo[:, k, a:b], k == 0, c == PART_C and k == NCH - 1)

            def act_ready(T, k):
                if k % 4 == 0:
                    pe.wait_ge(actlo_done, 2 * T + 1 + k // 4)

            def turn_u(T, first=False):
                pe.wait_ge(gated, 4 * T + 4)
                if not first:
                    pe.wait_ge(utlo_done, T)
                pe.transpose(utp[:, 0:P], u_sb[:, :], ident[:, :]).then_inc(ut_done, 1)

            def lora_out(T, s, cols, c, rows_):
                a, b = dense_cols(cols, c)
                pe.wait_ge(utlo_done, T + 1)
                three(acc(c, s)[:, 0:b - a], ut_hi[0:rows_, :], ut_lo[0:rows_, :], lb_hi[0:rows_, a:b],
                      lb_lo[0:rows_, a:b], False, True, skip=(c == PART_C)).then_inc(part_done[c], 1)

            def mlp(m, rhs):
                w = pk[:, PK_W0 + EMB * m:PK_W0 + EMB * (m + 1)]
                pe.matmul(utp[:, NB * m:NB * m + NB], w, rhs, start=True, stop=True).then_inc(mlp_mm, 1)

            pe.wait_ge(consts, 1)
            for _ in range(WARM):
                pe.matmul(acc_b[:, 0:P], ones[:, :], ones[:, :], start=True, stop=True)

            pe.wait_ge(s_pk, 16)
            pe.matmul(acc_b[0:NB, 0:CH], pk[:, PK_C:PK_C + NB], pk[:, PK_CW:PK_CW + CH],
                      start=True, stop=True).then_inc(ctx_mm, 1)
            mlp(0, pk[:, PK_C:PK_C + NB])
            pe.wait_ge(mlp_h, 1)
            mlp(1, hg[:, 0, :])
            pe.wait_ge(mlp_h, 2)
            pe.matmul(utp[0:NB, 2 * NB:2 * NB + KMIX], hg[:, 1, :], pk[:, PK_W2:PK_W2 + KMIX],
                      start=True, stop=True).then_inc(mlp_mm, 1)
            conv(0, 0, 0, first=True)
            pe.wait_ge(consts, 3)
            pe.wait_ge(att_op, 5)
            pe.transpose(utp[:, 2 * P:2 * P + NB], att_rep[:, :, :].rearrange("b o k -> b (o k)"),
                         ident[0:NB, 0:NB]).then_inc(att_t, 1)
            pe.wait_ge(s_mixw, 32)
            pe.wait_ge(att_diag_done, 1)

            def mix_kernels(m):
                if m >= 2:
                    pe.wait_ge(agg_read, 2 * (m - 1))
                bank = (acc_a if m % 2 else acc_c)[:, 1, :]
                pe.matmul(bank, mixw_sb[:, m, :, :].rearrange("p n i -> p (n i)"),
                          att_diag[:, :, :].rearrange("p o b -> p (o b)"), start=True, stop=True).then_inc(agg_mm, 1)

            mix_kernels(0)
            pe.wait_ge(s_bk, 16)
            pe.matmul(utp[0:NB, 3 * P:3 * P + CH], att_all[0:KMIX, :], bk[:, :], start=True, stop=True).then_inc(aggb_mm, 1)
            mix_kernels(1)

            pe.wait_ge(ctx_sum, 1)
            for k in range(NCH):
                act_ready(0, k)
                pe.wait_ge(wlo_done, k + 1)
                for c in (PART_C, PART_A, PART_B):
                    ins = dense(0, COLS0, c, k)
                    if k == NCH - 1 and c == PART_C:
                        ins.then_inc(hid_done, 1)
            conv(1, 1, 0)
            mix_kernels(2)
            mix_kernels(3)
            pe.wait_ge(aggb_copied, 1)
            turn_u(0, first=True)
            pe.wait_ge(lblo_done, 1)
            for c in (PART_C, PART_A, PART_B):
                lora_out(0, 0, COLS0, c, RANK + 1)

            def step(T, s, pair, cols, rows_, following, c_free=None):
                for k in range(NCH):
                    act_ready(T, k)
                    if k == 0:
                        if c_free is None:
                            pe.wait_ge(res_done[PART_C], T - 1)
                        else:
                            pe.wait_ge(*c_free)
                    ins = dense(s, cols, PART_C, k)
                ins.then_inc(hid_done, 1)
                if c_free is None:
                    pe.wait_ge(res_done[PART_A], T - 1)
                for k in range(NCH):
                    dense(s, cols, PART_A, k)
                    if k == NCH - 2:
                        turn_u(T)
                if following is not None:
                    following(T + 1, 1 - s, pair + s)
                lora_out(T, s, cols, PART_C, rows_)
                lora_out(T, s, cols, PART_A, rows_)
                pe.wait_ge(res_done[PART_B], T)
                for k in range(NCH):
                    dense(s, cols, PART_B, k)
                lora_out(T, s, cols, PART_B, rows_)

            def step0(T, s, pair, c_free=None):
                step(T, s, pair, COLS0, RANK + 1, conv, c_free)

            def step1(T, s, pair):
                step(T, s, pair, COLS1, P, mix)

            step0(1, 1, 0, c_free=(agg_read, 2 * CH // OQ))
            step0(2, 0, 1)
            loop_steps(pe, 3, TILES - 4, step0)
            T = TILES - 1
            for k in range(NCH):
                act_ready(T, k)
                if k == 0:
                    pe.wait_ge(res_done[PART_C], T - 1)
                ins = dense(1, COLS0, PART_C, k)
            ins.then_inc(hid_done, 1)
            mix(TILES, 0, TILES // 2)
            pe.wait_ge(res_done[PART_A], T - 1)
            pe.wait_ge(res_done[PART_B], T)
            for k in range(NCH):
                dense(1, COLS0, PART_A, k)
                dense(1, COLS0, PART_B, k).then_inc(w_free, 1)
                if k == 1:
                    turn_u(T)
            for c in (PART_C, PART_A, PART_B):
                lora_out(T, 1, COLS0, c, RANK + 1)

            T = TILES
            pe.wait_ge(res_done[PART_C], T - 1)
            pe.wait_ge(res_done[PART_A], T - 1)
            for k in range(NCH):
                act_ready(T, k)
                pe.wait_ge(wlo_done, NCH + k + 1)
                for c in (PART_C, PART_A, PART_B):
                    if k == 0 and c == PART_B:
                        pe.wait_ge(res_done[PART_B], T)
                    ins = dense(0, COLS1, c, k)
                    if k == NCH - 1 and c == PART_C:
                        ins.then_inc(hid_done, 1)
            mix(T + 1, 1, T // 2)
            turn_u(T)
            pe.wait_ge(lblo_done, 2)
            for c in (PART_C, PART_A, PART_B):
                lora_out(T, 0, COLS1, c, P)

            loop_steps(pe, TILES + 1, TILES - 2, step1)
            step(LAST, 1, LAST // 2, COLS1, P, None)


_OUT = (NB, CH, D)


def _layout(inp):
    a = {k: np.asarray(v) for k, v in inp.items()}
    x = a["x"]
    xp = np.pad(x, ((0, 0), (0, 0), (PAD, PAD))).reshape(TILES, 2, GROUPS, GC, QX, POS)[..., ::-1]
    xblk = xp.transpose(0, 3, 5, 1, 2, 4).reshape(TILES, P, 2 * GROUPS * QX)
    toep = np.zeros((GROUPS, GC, TOEP, GC), np.float32)
    w = a["L0_cond_weight"].reshape(GROUPS, GC, GC, TAPS)[..., ::-1]
    toep[:, :, POS - 1:POS - 1 + TAPS, :] = w.transpose(0, 2, 3, 1)
    wcat0 = np.concatenate([a["L0_ffn_W"], a["L0_ffn_A"], a["L0_ffn_gate_w"]]).T.reshape(P, NCH, W0COLS)
    lora_a = a["L1_ffn_lora_A"].transpose(0, 2, 1).reshape(EXP * ER, D)
    wcat1 = np.concatenate([a["L1_ffn_W_base"], lora_a, a["L1_ffn_W_router"]]).T
    wcat1 = wcat1.reshape(NCH, P, W1COLS).transpose(1, 0, 2)
    bcat0 = np.concatenate([a["L0_ffn_B"].T, a["L0_ffn_b"][None]])
    pack = np.concatenate([a["cond_128"].T, a["L0_cond_c_weight"].T, a["L1_cond_W0"], a["L1_cond_W1"],
                           a["L1_cond_W2"], a["L1_cond_b0"][:, None], a["L1_cond_b1"][:, None]], axis=1)
    rows = np.concatenate([a["fside_S_0"], a["L0_ffn_gate_b"], a["L1_cond_b2"], a["L1_ffn_b_router"]])
    mixw = a["L1_cond_weight"].reshape(KMIX, CH // OQ, OQ, CH).transpose(2, 0, 1, 3).reshape(P, CH // OQ * CH)
    return {"x": x, "xblk": xblk, "toep": toep, "wcat0": wcat0, "bcat0": bcat0, "wcat1": wcat1,
            "bcat1": a["L1_ffn_lora_B"].reshape(P, D), "b_base": a["L1_ffn_b_base"], "pack": pack, "rows": rows,
            "mixw": mixw, "bias_k": a["L1_cond_bias_k"]}


def kernel(**inputs):
    import concourse.bacc as bacc
    from concourse.bass_utils import run_bass_kernel_spmd

    nc = bacc.Bacc("TRN2", target_bir_lowering=False, num_devices=1)
    arrays, aps = {}, {}
    for name, a in _layout(inputs).items():
        a = np.ascontiguousarray(a)
        arrays[f"in_{name}"] = a
        aps[name] = nc.dram_tensor(f"in_{name}", a.shape, mybir.dt.from_np(a.dtype), kind="ExternalInput").ap()
    out = nc.dram_tensor("out_dram", _OUT, F32, kind="ExternalOutput").ap()
    build(nc, out=out, **aps)
    return run_bass_kernel_spmd(nc, [arrays], core_ids=[0]).results[0]["out_dram"]
```

```python
from contextlib import ExitStack

import numpy as np

import concourse.bass as bass
from concourse import mybir

F32 = mybir.dt.float32
F32R = mybir.dt.float32r
ALU = mybir.AluOpType
ACT = mybir.ActivationFunctionType
AX_X = mybir.AxisListType.X

P = 128
NB, CH, D = 32, 64, 1024
TILES = NB * CH // P
NCH = D // P
BANK = 512
GROUPS, TAPS, PAD = 4, 9, 4
GC = CH // GROUPS
POS = P // GC
QB = D // POS
QX = QB + 1
TOEP = 2 * POS + POS - 1
RANK = 64
RANKS = (8, 16, 32, 64)
HID0 = RANK + len(RANKS)
BIAS_HI, BIAS_LO = 64, 96
ROWS0 = BIAS_LO + 1
EXP, ER = 8, 16
HID1 = EXP * ER + EXP
W0COLS, W1COLS = D + HID0, D + HID1
PART_A, PART_B, PART_C = range(3)
COLS0 = [(0, 364), (364, 728), (728, W0COLS)]
COLS1 = [(0, 388), (388, 776), (776, W1COLS)]
KMIX = 8
OQ = P // (2 * KMIX)
MIXES = CH // OQ
EMB = 128
WARM, WARM_WEIGHTS = 7, 6

PK_C = 0
PK_CW = PK_C + NB
PK_W0 = PK_CW + CH
PK_W1 = PK_W0 + EMB
PK_W2 = PK_W1 + EMB
PK_B0 = PK_W2 + KMIX
PACK = PK_B0 + 2
RW_FS = 0
RW_GB = RW_FS + CH
RW_B2 = RW_GB + len(RANKS)
RW_RB = RW_B2 + KMIX
ROW = RW_RB + EXP


def build(nc, x, xblk, toep, wcat0, bcat0, bias0, wcat1, bcat1, b_base, pack, rows, mixw, bias_k, out):
    x_t = x.rearrange("(t n) c h -> t (n c) h", n=2)
    out_t = out.rearrange("(t n) c h -> t (n c) h", n=2)
    x1_t = nc.dram_tensor("x1_scratch", (TILES, P, D), F32, kind="Internal").ap()
    ctx_d = nc.dram_tensor("ctx_scratch", (NB, CH), F32, kind="Internal").ap()
    aggb_d = nc.dram_tensor("aggb_scratch", (NB, CH), F32, kind="Internal").ap()

    with ExitStack() as ctx:
        def sb(name, shape, dt=F32):
            return ctx.enter_context(nc.sbuf_tensor(name, shape, dt))

        def psum(name, shape):
            return ctx.enter_context(nc.psum_tensor(name, shape, F32))

        def sem(name):
            return ctx.enter_context(nc.semaphore(name))

        w_hi = sb("w_hi", [P, NCH, W1COLS], F32R)
        w_lo = sb("w_lo", [P, NCH, W1COLS], F32R)
        w_raw = sb("w_raw", [P, NCH, W1COLS])
        lb_hi = sb("lb_hi", [P, D], F32R)
        lb_lo = sb("lb_lo", [P, D], F32R)
        lb_raw = sb("lb_raw", [P, D])
        filt = sb("filt", [P, GROUPS, 2 * P])
        agg = sb("agg", [P, TILES, 2, CH])
        ctx_row = sb("ctx_row", [P, TILES, P])
        aggb_row = sb("aggb_row", [P, TILES, P])
        bbase = sb("bbase", [P, D])
        xs = [sb("xs0", [P, D]), sb("xs1", [P, D])]
        blk = [sb("blk0", [P, 2 * GROUPS * QX]), sb("blk1", [P, 2 * GROUPS * QX])]
        mixed = sb("mixed", [P, NCH, P])
        act_hi = sb("act_hi", [P, 2, NCH, P], F32R)
        act_lo = sb("act_lo", [P, 2, NCH, P], F32R)
        u_sb = sb("u_sb", [P, P])
        ut_hi = sb("ut_hi", [P, P], F32R)
        ut_lo = sb("ut_lo", [P, P], F32R)
        pk = sb("pk", [P, PACK])
        rw = sb("rw", [P, ROW])
        bk = sb("bk", [KMIX, CH])
        mixw_sb = sb("mixw_sb", [P, MIXES, 2 * CH])
        diag = sb("diag", [P, 2 * OQ])
        ident = sb("ident", [P, P])
        ones = sb("ones", [P, P])
        inv_k = sb("inv_k", [P, EXP])
        hg = sb("hg", [P, 2, NB])
        ctx_sb = sb("ctx_sb", [NB, CH])
        aggb_sb = sb("aggb_sb", [NB, CH])
        att = sb("att", [NB, 3, KMIX])
        att_rep = sb("att_rep", [NB, 2 * OQ, KMIX])
        stat = sb("stat", [NB, 4])
        att_all = sb("att_all", [P, NB])
        att_diag = sb("att_diag", [P, OQ, TILES])
        sc = sb("sc", [P, 8])
        pm = sb("pm", [P, 8])
        keep = sb("keep", [P, 4])
        kw = sb("kw", [P, 8])
        ex = sb("ex", [P, 4])
        st = sb("st", [P, 8])
        gs = sb("gs", [P, 4, EXP])

        acc_a = psum("acc_a", [P, 2, BANK])
        acc_b = psum("acc_b", [P, BANK])
        acc_c = psum("acc_c", [P, 2, BANK])
        mixp = psum("mixp", [P, 2, BANK])
        utp = psum("utp", [P, BANK])

        s_pk = sem("s_pk")
        s_rw = sem("s_rw")
        s_bk = sem("s_bk")
        s_mixw = sem("s_mixw")
        s_bbase = sem("s_bbase")
        s_filt = [sem(f"s_filt{g}") for g in range(GROUPS)]
        s_lb = sem("s_lb")
        s_bias0 = sem("s_bias0")
        ctx_second = sem("ctx_second")
        ctx_rest = sem("ctx_rest")
        aggb_loaded = sem("aggb_loaded")
        w_loaded = [sem(f"w_loaded{k}") for k in range(NCH)]
        blk_loaded = [sem("blk_loaded0"), sem("blk_loaded1")]
        xs_loaded = [sem("xs_loaded0"), sem("xs_loaded1")]
        ctx_stored = sem("ctx_stored")
        aggb_stored = sem("aggb_stored")
        xs_stored = [sem("xs_stored0"), sem("xs_stored1")]
        whi_done = sem("whi_done")
        wlo_done = sem("wlo_done")
        lbhi_done = sem("lbhi_done")
        lblo_done = sem("lblo_done")
        bias_split = sem("bias_split")
        acthi_done = sem("acthi_done")
        actlo_done = sem("actlo_done")
        uthi_done = sem("uthi_done")
        utlo_done = sem("utlo_done")
        uthi_second = sem("uthi_second")
        mix_done = sem("mix_done")
        sum_done = sem("sum_done")
        hid_done = sem("hid_done")
        gate_op = sem("gate_op")
        gate_max = sem("gate_max")
        exp_done = sem("exp_done")
        gated = sem("gated")
        ut_done = sem("ut_done")
        part_done = [sem("part_a_done"), sem("part_b_done"), sem("part_c_done")]
        biased = sem("biased")
        res_done = [sem("res_a_done"), sem("res_b_done"), sem("res_c_done")]
        w_free = sem("w_free")
        consts = sem("consts")
        ctx_mm = sem("ctx_mm")
        ctx_sum = sem("ctx_sum")
        mlp_mm = sem("mlp_mm")
        mlp_h = sem("mlp_h")
        att_op = sem("att_op")
        att_exp = sem("att_exp")
        att_t = sem("att_t")
        att_copied = sem("att_copied")
        att_diag_done = sem("att_diag_done")
        agg_mm = sem("agg_mm")
        agg_read = sem("agg_read")
        aggb_mm = sem("aggb_mm")
        aggb_copied = sem("aggb_copied")

        block = ctx.enter_context(nc.Block())
        LAST = 2 * TILES - 1
        GATE0, GATE1 = 7, 6
        N_CONSTS = 10 + EXP

        def hi(part):
            return part.bitcast(F32)

        def acc(c, s):
            return (acc_a[:, s, :], acc_b[:, :], acc_c[:, s, :])[c]

        def dense_cols(cols, c):
            return cols[c][0], min(cols[c][1], D)

        def loop_steps(eng, first, count, body):
            with eng.Fori(0, count // 2) as i:
                body(2 * i + first, first % 2, i + first // 2)
                body(2 * i + (first + 1), (first + 1) % 2, i + (first + 1) // 2)

        @block.sync
        def _(sp):
            def rows_of(dram, t):
                return dram[bass.ds(t, 1)].rearrange("a p h -> (a p) h")

            def load_blocks(t, s):
                sp.dma_start(blk[s][:, :], rows_of(xblk, t)).then_inc(blk_loaded[s], 16)

            def load_w(k, layer):
                wcat, cols = ((wcat0, W0COLS), (wcat1, W1COLS))[layer]
                sp.dma_start(w_raw[:, k, 0:cols], wcat[:, k, :]).then_inc(w_loaded[k], 16)

            def load_x(t, s):
                sp.dma_start(xs[s][:, :], rows_of(x_t, t)).then_inc(xs_loaded[s], 16)

            def load_x1(t, s):
                sp.dma_start(blk[s][:, 0:D], rows_of(x1_t, t)).then_inc(blk_loaded[s], 16)

            def store(dram, t, T, s):
                for c in range(3):
                    sp.wait_ge(res_done[c], T + 1)
                sp.dma_start(rows_of(dram, t), xs[s][:, :]).then_inc(xs_stored[s], 16)

            sp.dma_start(pk[:, :], pack).then_inc(s_pk, 16)
            load_blocks(0, 0)
            for g in range(GROUPS):
                src = bass.AP(toep.tensor, g * GC * TOEP * GC, [[TOEP * GC, GC], [GC, POS], [1, 2 * P]])
                sp.dma_start(filt[:, g, :], src).then_inc(s_filt[g], 16)
            load_w(0, 0)
            load_w(1, 0)
            load_w(2, 0)
            sp.wait_ge(ctx_sum, 1)
            sp.dma_start(ctx_d, ctx_sb[:, :]).then_inc(ctx_stored, 16)
            load_w(3, 0)
            load_w(4, 0)
            sp.wait_ge(ctx_stored, 16)
            ctx_rows = ctx_d.rearrange("(t n) c -> t (n c)", n=2)
            sp.dma_start(ctx_row[:, 1, :], ctx_rows[1].partition_broadcast(P)).then_inc(ctx_second, 16)
            for k in range(5, NCH):
                load_w(k, 0)
            sp.dma_start(bbase[BIAS_HI:ROWS0, :], bias0).then_inc(s_bias0, 16)
            sp.dma_start(lb_raw[:, :], bcat0).then_inc(s_lb, 16)
            load_blocks(1, 1)
            sp.dma_start(mixw_sb[:, :, :], mixw).then_inc(s_mixw, 16)
            load_x(0, 0)
            sp.dma_start(ctx_row[:, 2:TILES, :].rearrange("p t c -> p (t c)"),
                         ctx_rows[2:TILES].rearrange("t c -> (t c)").partition_broadcast(P)).then_inc(ctx_rest, 16)
            sp.wait_ge(mix_done, 2)
            load_blocks(2, 0)
            load_x(1, 1)
            for k in range(NCH):
                sp.wait_ge(wlo_done, k + 1)
                load_w(k, 1)
            sp.wait_ge(lblo_done, 1)
            sp.dma_start(lb_raw[:, :], bcat1).then_inc(s_lb, 16)
            sp.wait_ge(aggb_copied, 1)
            sp.dma_start(aggb_d, aggb_sb[:, :]).then_inc(aggb_stored, 16)
            sp.wait_ge(aggb_stored, 16)
            sp.dma_start(aggb_row[:, :, :].rearrange("p t c -> p (t c)"),
                         aggb_d.rearrange("b c -> (b c)").partition_broadcast(P)).then_inc(aggb_loaded, 16)
            sp.wait_ge(bias_split, 1)
            sp.dma_start(bbase[:, :], b_base.partition_broadcast(P)).then_inc(s_bbase, 16)

            def step0(T, s, pair):
                sp.wait_ge(mix_done, 2 * T + 2)
                load_blocks(T + 2, s)
                store(x1_t, T - 1, T - 1, 1 - s)
                sp.wait_ge(xs_stored[1 - s], 16 * pair + 16 * s)
                load_x(T + 1, 1 - s)

            loop_steps(sp, 1, TILES - 4, step0)
            step0(TILES - 3, 1, (TILES - 3) // 2)
            T = TILES - 2
            sp.wait_ge(mix_done, 2 * T + 2)
            load_x1(0, 0)
            store(x1_t, T - 1, T - 1, 1)
            sp.wait_ge(xs_stored[1], 16 * (T // 2))
            load_x(T + 1, 1)
            T = TILES - 1
            sp.wait_ge(mix_done, 2 * T + 2)
            load_x1(1, 1)
            store(x1_t, T - 1, T - 1, 0)
            store(x1_t, T, T, 1)
            for s in range(2):
                sp.wait_ge(xs_stored[s], 16 * (TILES // 2))

            def step1(T, s, pair):
                for c in range(3):
                    sp.wait_ge(res_done[c], T)
                load_x1(T + 1 - TILES, 1 - s)
                store(out_t, T - 1 - TILES, T - 1, 1 - s)

            loop_steps(sp, TILES + 1, TILES - 2, step1)
            store(out_t, TILES - 2, LAST - 1, 0)
            for c in (PART_C, PART_A, PART_B):
                a, b = dense_cols(COLS1, c)
                sp.wait_ge(res_done[c], LAST + 1)
                sp.dma_start(out_t[TILES - 1, :, a:b], xs[1][:, a:b]).then_inc(xs_stored[1], 16)
            sp.wait_ge(xs_stored[0], 16 * TILES)
            sp.wait_ge(xs_stored[1], 16 * (TILES + 2))

        @block.gpsimd
        def _(pool):
            pool.memset(ones[:, :], 1.0).then_inc(consts, 1)
            pool.memset(ident[:, :], 0.0).then_inc(consts, 1)
            pool.dma_start(rw[:, :], rows.partition_broadcast(P)).then_inc(s_rw, 16)
            pool.wait_ge(consts, 2)
            pool.affine_select(out=ident[:, :], in_=ident[:, :], compare_op=ALU.not_equal, fill=1.0, base=0,
                               pattern=[[-1, P]], channel_multiplier=1).then_inc(consts, 1)
            pool.affine_select(out=diag[:, :], in_=ones[:, 0:2 * OQ], compare_op=ALU.is_ge, fill=0.0, base=0,
                               pattern=[[-KMIX, 2 * OQ]], channel_multiplier=1).then_inc(consts, 1)
            pool.wait_ge(consts, 4)
            pool.affine_select(out=diag[:, :], in_=diag[:, :], compare_op=ALU.is_ge, fill=0.0, base=KMIX - 1,
                               pattern=[[KMIX, 2 * OQ]], channel_multiplier=-1).then_inc(consts, 1)
            pool.dma_start(bk[:, :], bias_k).then_inc(s_bk, 16)
            for k in range(EXP):
                pool.memset(inv_k[:, k:k + 1], 1.0 / (k + 1)).then_inc(consts, 1)
            pool.memset(keep[:, 0:1], 1.0).then_inc(consts, 1)
            pool.wait_ge(consts, N_CONSTS - 4)
            pool.memset(hi(ut_lo[RANK:P, :]), 0.0).then_inc(consts, 1)
            pool.wait_ge(consts, N_CONSTS - 3)
            pool.memset(hi(ut_lo[BIAS_HI:BIAS_HI + 1, :]), 1.0).then_inc(consts, 1)
            pool.wait_ge(consts, N_CONSTS - 2)
            pool.memset(hi(ut_lo[BIAS_LO:BIAS_LO + 1, :]), 1.0).then_inc(consts, 1)
            pool.wait_ge(consts, N_CONSTS - 1)
            pool.memset(agg[:, :, :, :], 0.0).then_inc(consts, 1)
            pool.wait_ge(consts, N_CONSTS)
            pool.wait_ge(lbhi_done, 1)
            pool.tensor_tensor(lb_lo[BIAS_LO:ROWS0, :], bbase[BIAS_LO:ROWS0, :], hi(lb_lo[BIAS_LO:ROWS0, :]),
                               ALU.subtract).then_inc(bias_split, 1)

        @block.scalar
        def _(act):
            def split_w(k, layer):
                cols = (W0COLS, W1COLS)[layer]
                act.wait_ge(w_loaded[k], 16 * layer + 16)
                if layer:
                    act.wait_ge(w_free, k + 1)
                act.copy(w_hi[:, k, 0:cols], w_raw[:, k, 0:cols]).then_inc(whi_done, 1)

            def gelu(m):
                act.wait_ge(mlp_mm, m + 1)
                act.activation(hg[:, m, :], utp[:, NB * m:NB * m + NB], ACT.Gelu,
                               bias=pk[:, PK_B0 + m:PK_B0 + m + 1]).then_inc(mlp_h, 1)

            def split_ut0(T, first=False):
                act.wait_ge(ut_done, T + 1)
                if not first:
                    act.wait_ge(part_done[PART_B], T)
                act.copy(ut_hi[:, :], utp[:, 0:P]).then_inc(uthi_done, 1)
                act.copy(ut_lo[0:RANK, :], utp[0:RANK, 0:P]).then_inc(uthi_second, 1)

            def split_act(T, s, per_bank, first=False, halves=(0, 1)):
                if not first:
                    act.wait_ge(part_done[PART_B], T - 1)
                for b in halves:
                    act.wait_ge(sum_done, 2 * T + (1 + b if per_bank else 2))
                    act.copy(act_hi[:, s, 4 * b:4 * b + 4, :], mixed[:, 4 * b:4 * b + 4, :]).then_inc(acthi_done, 1)

            def split_ut1(T):
                act.wait_ge(ut_done, T + 1)
                act.wait_ge(part_done[PART_B], T)
                act.copy(ut_hi[:, :], utp[:, 0:P]).then_inc(uthi_done, 1)

            def gate_exp(T):
                act.wait_ge(gate_max, T + 1)
                act.activation(ex[:, :], sc[:, 0:4], ACT.Exp, bias=st[:, 0:1],
                               accum_out=st[:, 1:2]).then_inc(exp_done, 1)

            gelu(0)
            gelu(1)
            act.wait_ge(att_op, 3)
            act.activation(att[:, 1, :], att[:, 0, :], ACT.Exp, bias=stat[:, 1:2],
                           accum_out=stat[:, 2:3]).then_inc(att_exp, 1)
            split_w(0, 0)
            split_act(0, 0, False, first=True, halves=(0,))
            split_w(1, 0)
            split_w(2, 0)
            split_act(0, 0, False, first=True, halves=(1,))
            for k in range(3, NCH):
                split_w(k, 0)
            act.wait_ge(s_bias0, 16)
            act.copy(lb_lo[BIAS_HI:ROWS0, :], bbase[BIAS_HI:ROWS0, :]).then_inc(lbhi_done, 1)
            def place_kernels(half):
                act.wait_ge(agg_mm, half + 1)
                src = (mixp[:, 0, :], acc_a[:, 1, :])[half].rearrange("p (o t) -> p t o", t=TILES)
                for n in range(2):
                    rows_ = slice(CH * n, CH * n + CH)
                    act.copy(agg[rows_, :, n, CH // 2 * half:CH // 2 * (half + 1)], src[rows_]).then_inc(agg_read, 1)

            act.wait_ge(s_lb, 16)
            act.copy(lb_hi[:, :], lb_raw[:, :]).then_inc(lbhi_done, 1)

            gate_exp(0)
            split_ut0(0, first=True)
            split_act(1, 1, False, first=True)
            act.wait_ge(consts, N_CONSTS)
            place_kernels(0)
            place_kernels(1)

            def step0(T, s, pair):
                gate_exp(T)
                split_ut0(T)
                split_act(T + 1, 1 - s, False)

            loop_steps(act, 1, TILES - 2, step0)
            T = TILES - 1
            gate_exp(T)
            split_ut0(T)
            split_act(TILES, 0, True)
            for k in range(NCH):
                split_w(k, 1)
            act.wait_ge(s_lb, 32)
            act.wait_ge(part_done[PART_B], TILES)
            act.copy(lb_hi[:, :], lb_raw[:, :]).then_inc(lbhi_done, 1)

            T = TILES
            split_ut1(T)
            split_act(T + 1, 1, True)

            def step1(T, s, pair):
                split_ut1(T)
                split_act(T + 1, 1 - s, True)

            loop_steps(act, TILES + 1, TILES - 2, step1)
            split_ut1(LAST)

        @block.vector
        def _(dve):
            def split_w(k, layer):
                cols = (W0COLS, W1COLS)[layer]
                dve.wait_ge(whi_done, NCH * layer + k + 1)
                dve.tensor_tensor(w_lo[:, k, 0:cols], w_raw[:, k, 0:cols],
                                  hi(w_hi[:, k, 0:cols]), ALU.subtract).then_inc(wlo_done, 1)

            def sum_conv(T, first=False, halves=(0, 1)):
                if not first:
                    dve.wait_ge(acthi_done, 2 * T)
                    dve.wait_ge(actlo_done, 2 * T)
                for n in halves:
                    dve.wait_ge(mix_done, 2 * T + n + 1)
                    row = ctx_row[:, bass.ds(T, 1), CH * n:CH * n + CH].to_broadcast([P, POS, CH])
                    dve.tensor_tensor(mixed[:, :, CH * n:CH * n + CH],
                                      mixp[:, n, :].rearrange("p (a c) -> p a c", c=CH), row,
                                      ALU.add).then_inc(sum_done, 1)

            def sum_mix(T, banks=(0, 1)):
                dve.wait_ge(acthi_done, 2 * T)
                dve.wait_ge(actlo_done, 2 * T)
                for b in banks:
                    dve.wait_ge(mix_done, 2 * T + b + 1)
                    row = aggb_row[:, bass.ds(T - TILES, 1), :].to_broadcast([P, 4, P])
                    dve.tensor_tensor(mixed[:, 4 * b:4 * b + 4, :],
                                      mixp[:, b, :].rearrange("p (a c) -> p a c", c=P), row,
                                      ALU.add).then_inc(sum_done, 1)

            def split_act(T, s, halves=(0, 1)):
                for b in halves:
                    dve.wait_ge(acthi_done, 2 * T + b + 1)
                    dve.tensor_tensor(act_lo[:, s, 4 * b:4 * b + 4, :], mixed[:, 4 * b:4 * b + 4, :],
                                      hi(act_hi[:, s, 4 * b:4 * b + 4, :]), ALU.subtract).then_inc(actlo_done, 1)

            def split_ut0(T):
                dve.wait_ge(uthi_done, T + 1)
                dve.tensor_tensor(ut_hi[RANK:P, :], utp[RANK:P, 0:P], hi(ut_hi[RANK:P, :]),
                                  ALU.subtract).then_inc(utlo_done, 1)

            def split_ut1(T):
                dve.wait_ge(uthi_done, T + 1)
                dve.tensor_tensor(ut_lo[:, :], utp[:, 0:P], hi(ut_hi[:, :]), ALU.subtract).then_inc(utlo_done, 1)

            def gate0(T, s, first=False):
                links = [0]

                def link(ins):
                    links[0] += 1
                    ins.then_inc(gate_op, 1)
                    dve.wait_ge(gate_op, GATE0 * T + links[0])

                hid = acc_c[:, s, D - COLS0[PART_C][0]:]
                dve.wait_ge(hid_done, T + 1)
                if not first:
                    dve.wait_ge(ut_done, T)
                link(dve.tensor_tensor(sc[:, 0:4], hid[:, RANK:HID0], rw[:, RW_GB:RW_GB + 4], ALU.add))
                link(dve.tensor_tensor_scan(pm[:, 0:4], sc[:, 0:4], sc[:, 0:4], -3.4e38, ALU.max, ALU.max))
                dve.tensor_scalar(st[:, 0:1], pm[:, 3:4], -1.0, None, ALU.mult).then_inc(gate_max, 1)
                link(dve.tensor_scalar(keep[:, 1:4], pm[:, 0:3], pm[:, 3:4], None, ALU.is_lt))
                dve.wait_ge(exp_done, T + 1)
                link(dve.reciprocal(st[:, 2:3], st[:, 1:2]))
                link(dve.reciprocal(st[:, 3:4], st[:, 2:3]))
                link(dve.tensor_tensor(st[:, 4:5], st[:, 2:3], st[:, 3:4], ALU.mult))
                link(dve.tensor_scalar(kw[:, 0:4], keep[:, :], st[:, 4:5], None, ALU.mult))
                r0 = 0
                for j, r in enumerate(RANKS):
                    dve.tensor_scalar(u_sb[:, :].rearrange("p (d r) -> p d r", d=2)[:, :, r0:r],
                                      hid[:, r0:r].unsqueeze(1).to_broadcast([P, 2, r - r0]),
                                      kw[:, j:j + 1], None, ALU.mult).then_inc(gated, 1)
                    r0 = r

            def gate1(T, s):
                n0 = GATE0 * TILES + (T - TILES) * GATE1
                links = [0]

                def link(ins):
                    links[0] += 1
                    ins.then_inc(gate_op, 1)
                    dve.wait_ge(gate_op, n0 + links[0])

                hid = acc_c[:, s, D - COLS1[PART_C][0]:]
                dve.wait_ge(hid_done, T + 1)
                dve.wait_ge(ut_done, T)
                link(dve.tensor_tensor(gs[:, 0, :], hid[:, P:HID1], rw[:, RW_RB:RW_RB + EXP], ALU.add))
                dve.nop(nofuse=True)
                link(dve.max(gs[:, 1, :], gs[:, 0, :]))
                link(dve.tensor_tensor_scan(gs[:, 2, :], ones[:, 0:EXP], gs[:, 1, :], -1.0, ALU.mult, ALU.add))
                link(dve.tensor_tensor(gs[:, 3, :], gs[:, 2, :], inv_k[:, :], ALU.mult))
                link(dve.tensor_reduce(st[:, 0:1], gs[:, 3, :], AX_X, ALU.max))
                link(dve.tensor_scalar(sc[:, :], gs[:, 0, :], st[:, 0:1], 0.0, ALU.subtract, ALU.max))
                dve.tensor_tensor(u_sb[:, :].rearrange("p (e r) -> p e r", r=ER),
                                  hid[:, 0:P].rearrange("p (e r) -> p e r", r=ER),
                                  sc[:, :].unsqueeze(2).to_broadcast([P, EXP, ER]), ALU.mult).then_inc(gated, 4)

            def res0(T, s, pair, c):
                a, b = dense_cols(COLS0, c)
                dve.wait_ge(xs_loaded[s], 16 * pair + 16)
                dve.wait_ge(part_done[c], T + 1)
                dve.tensor_tensor(xs[s][:, a:b], acc(c, s)[:, 0:b - a], xs[s][:, a:b], ALU.add).then_inc(res_done[c], 1)

            def res1(T, s, pair, c):
                a, b = dense_cols(COLS1, c)
                dve.wait_ge(part_done[c], T + 1)
                dve.wait_ge(xs_stored[s], 16 * pair)
                dve.tensor_tensor(xs[s][:, a:b], acc(c, s)[:, 0:b - a], bbase[:, a:b], ALU.add).then_inc(biased, 1)
                order = (PART_C, PART_A, PART_B).index(c)
                dve.wait_ge(biased, 3 * (T - TILES) + order + 1)
                dve.tensor_tensor(xs[s][:, a:b], xs[s][:, a:b], blk[s][:, a:b], ALU.add).then_inc(res_done[c], 1)

            dve.wait_ge(ctx_mm, 1)
            dve.wait_ge(s_rw, 16)
            dve.tensor_tensor(ctx_sb[:, :], acc_b[0:NB, 0:CH], rw[0:NB, RW_FS:RW_FS + CH], ALU.add).then_inc(ctx_sum, 1)
            dve.tensor_tensor(ctx_row[:, 0, :].rearrange("p (n c) -> p n c", n=2),
                              acc_b[:, CH:3 * CH].rearrange("p (n c) -> p n c", n=2),
                              rw[:, RW_FS:RW_FS + CH].unsqueeze(1).to_broadcast([P, 2, CH]), ALU.add).then_inc(ctx_sum, 1)

            dve.wait_ge(mlp_mm, 3)
            dve.tensor_tensor(att[:, 0, :], utp[0:NB, 2 * NB:2 * NB + KMIX], rw[0:NB, RW_B2:RW_B2 + KMIX],
                              ALU.add).then_inc(att_op, 1)
            dve.wait_ge(att_op, 1)
            dve.tensor_reduce(stat[:, 0:1], att[:, 0, :], AX_X, ALU.max).then_inc(att_op, 1)
            dve.wait_ge(att_op, 2)
            dve.tensor_scalar(stat[:, 1:2], stat[:, 0:1], -1.0, None, ALU.mult).then_inc(att_op, 1)
            dve.wait_ge(ctx_sum, 2)
            sum_conv(0, first=True, halves=(0,))
            dve.wait_ge(att_exp, 1)
            dve.reciprocal(stat[:, 3:4], stat[:, 2:3]).then_inc(att_op, 1)
            dve.wait_ge(att_op, 4)
            dve.tensor_scalar(att_rep[:, :, :], att[:, 1, :].unsqueeze(1).to_broadcast([NB, 2 * OQ, KMIX]),
                              stat[:, 3:4], None, ALU.mult).then_inc(att_op, 1)
            sum_conv(0, first=True, halves=(1,))
            split_w(0, 0)
            split_act(0, 0, halves=(0,))
            split_w(1, 0)
            split_w(2, 0)
            split_act(0, 0, halves=(1,))
            dve.wait_ge(att_t, 1)
            dve.tensor_copy(att_all[:, :], utp[:, 2 * P:2 * P + NB]).then_inc(att_copied, 1)
            split_w(3, 0)
            dve.wait_ge(att_copied, 1)
            dve.wait_ge(consts, 5)
            for n in range(2):
                rows_ = slice(CH * n, CH * n + CH)
                dve.tensor_tensor(att_diag[rows_, :, :],
                                  diag[rows_, OQ * n:OQ * n + OQ].unsqueeze(2).to_broadcast([CH, OQ, TILES]),
                                  att_all[rows_, :].rearrange("p (t n) -> p n t", n=2)[:, n:n + 1, :].to_broadcast([CH, OQ, TILES]),
                                  ALU.mult).then_inc(att_diag_done, 1)
            split_w(4, 0)
            for k in range(5, NCH):
                split_w(k, 0)
            dve.wait_ge(aggb_mm, 1)
            dve.tensor_copy(aggb_sb[:, :], utp[0:NB, 3 * P:3 * P + CH]).then_inc(aggb_copied, 1)
            dve.wait_ge(lbhi_done, 2)
            dve.tensor_tensor(lb_lo[0:RANK, :], lb_raw[0:RANK, :], hi(lb_hi[0:RANK, :]),
                              ALU.subtract).then_inc(lblo_done, 1)

            dve.wait_ge(consts, N_CONSTS)
            gate0(0, 0, first=True)
            dve.wait_ge(ctx_second, 16)
            sum_conv(1, halves=(0,))
            split_ut0(0)
            sum_conv(1, halves=(1,))
            split_act(1, 1)
            dve.wait_ge(ctx_rest, 16)
            for c in (PART_C, PART_A, PART_B):
                res0(0, 0, 0, c)

            def step0(T, s, pair):
                gate0(T, s)
                split_ut0(T)
                sum_conv(T + 1)
                split_act(T + 1, 1 - s)
                for c in (PART_C, PART_A, PART_B):
                    res0(T, s, pair, c)

            loop_steps(dve, 1, TILES - 2, step0)
            T = TILES - 1
            gate0(T, 1)
            dve.wait_ge(aggb_loaded, 16)
            sum_mix(TILES)
            split_act(TILES, 0)
            split_w(0, 1)
            split_ut0(T)
            for k in range(1, 3):
                split_w(k, 1)
            res0(T, 1, T // 2, PART_B)
            for k in range(3, 5):
                split_w(k, 1)
            res0(T, 1, T // 2, PART_C)
            res0(T, 1, T // 2, PART_A)
            for k in range(5, NCH):
                split_w(k, 1)
            dve.wait_ge(lbhi_done, 3)
            dve.tensor_tensor(lb_lo[:, :], lb_raw[:, :], hi(lb_hi[:, :]), ALU.subtract).then_inc(lblo_done, 1)

            dve.wait_ge(s_bbase, 16)
            T = TILES
            gate1(T, 0)
            sum_mix(T + 1, banks=(0,))
            split_ut1(T)
            sum_mix(T + 1, banks=(1,))
            split_act(T + 1, 1)
            for c in (PART_C, PART_A, PART_B):
                res1(T, 0, T // 2, c)

            def step1(T, s, pair):
                gate1(T, s)
                split_ut1(T)
                sum_mix(T + 1)
                split_act(T + 1, 1 - s)
                for c in (PART_C, PART_A, PART_B):
                    res1(T, s, pair, c)

            loop_steps(dve, TILES + 1, TILES - 2, step1)
            gate1(LAST, 1)
            split_ut1(LAST)
            dve.wait_ge(xs_stored[1], 16 * (LAST // 2))
            dve.tensor_tensor(xs[1][:, :], blk[1][:, 0:D], bbase[:, :], ALU.add).then_inc(biased, 1)
            dve.wait_ge(biased, 3 * (TILES - 1) + 1)
            for c in (PART_C, PART_A, PART_B):
                a, b = dense_cols(COLS1, c)
                dve.wait_ge(part_done[c], LAST + 1)
                dve.tensor_tensor(xs[1][:, a:b], acc(c, 1)[:, 0:b - a], xs[1][:, a:b], ALU.add).then_inc(res_done[c], 1)

        @block.tensor
        def _(pe):
            def three(dst, l_hi, l_lo, r_hi, r_lo, start, stop, skip=False):
                pe.matmul(dst, l_hi, r_hi, start=start, stop=False, skip_group_check=skip)
                pe.matmul(dst, l_hi, r_lo, start=False, stop=False, skip_group_check=skip)
                return pe.matmul(dst, l_lo, r_hi, start=False, stop=stop, skip_group_check=skip)

            def conv_group(s, n, g):
                at = (n * GROUPS + g) * QX
                dst = mixp[:, n, :].rearrange("p (a c) -> p a c", c=CH)[:, :, g * GC:(g + 1) * GC]
                for side in range(2):
                    taps = filt[:, g, (1 - side) * P:(2 - side) * P].rearrange("p (a c) -> p a c", c=GC)
                    ins = pe.matmul(dst, blk[s][:, at + side:at + side + QB], taps,
                                    start=(side == 0), stop=(side == 1))
                return ins

            def conv(T, s, pair, between=None):
                pe.wait_ge(blk_loaded[s], 16 * pair + 16)
                pe.wait_ge(sum_done, 2 * T)
                for n in range(2):
                    for g in range(GROUPS):
                        ins = conv_group(s, n, g)
                        if n == 1 and g == 1 and between is not None:
                            between()
                    ins.then_inc(mix_done, 1)

            def mix(T, s, pair, between=None):
                pe.wait_ge(blk_loaded[s], 16 * pair + 16)
                pe.wait_ge(sum_done, 2 * T)
                mat = agg[:, bass.ds(T - TILES, 1), :, :].rearrange("p t n o -> p (t n o)")
                for b in range(2):
                    for c in range(4):
                        k = 4 * b + c
                        ins = pe.matmul(mixp[:, b, c * P:(c + 1) * P], blk[s][:, k * P:(k + 1) * P], mat,
                                        start=True, stop=True)
                        if b == 1 and c == 1 and between is not None:
                            between()
                    ins.then_inc(mix_done, 1)

            def dense(s, cols, c, k):
                a, b = cols[c]
                return three(acc(c, s)[:, 0:b - a], act_hi[:, s, k, :], act_lo[:, s, k, :],
                             w_hi[:, k, a:b], w_lo[:, k, a:b], k == 0, c == PART_C and k == NCH - 1)

            def act_ready(T, k):
                if k % 4 == 0:
                    pe.wait_ge(actlo_done, 2 * T + 1 + k // 4)

            def turn_u(T, first=False):
                pe.wait_ge(gated, 4 * T + 4)
                if not first:
                    pe.wait_ge(utlo_done, T)
                pe.transpose(utp[:, 0:P], u_sb[:, :], ident[:, :]).then_inc(ut_done, 1)

            def lora0(T, s, c):
                a, b = dense_cols(COLS0, c)
                dst = acc(c, s)[:, 0:b - a]
                pe.wait_ge(utlo_done, T + 1)
                pe.matmul(dst, ut_hi[:, :], lb_hi[:, a:b], start=False, stop=False, skip_group_check=(c == PART_C))
                pe.wait_ge(uthi_second, T + 1)
                pe.matmul(dst, ut_lo[0:ROWS0, :], lb_lo[0:ROWS0, a:b], start=False, stop=True,
                          skip_group_check=(c == PART_C)).then_inc(part_done[c], 1)

            def lora1(T, s, c):
                a, b = dense_cols(COLS1, c)
                pe.wait_ge(utlo_done, T + 1)
                three(acc(c, s)[:, 0:b - a], ut_hi[:, :], ut_lo[:, :], lb_hi[:, a:b],
                      lb_lo[:, a:b], False, True, skip=(c == PART_C)).then_inc(part_done[c], 1)

            def mlp(m, rhs):
                w = pk[:, PK_W0 + EMB * m:PK_W0 + EMB * (m + 1)]
                pe.matmul(utp[:, NB * m:NB * m + NB], w, rhs, start=True, stop=True).then_inc(mlp_mm, 1)

            def keep_warm(count):
                for _ in range(count):
                    pe.matmul(acc_a[:, 1, 0:P], ones[:, :], ones[:, :], start=True, stop=True)

            pe.wait_ge(consts, 1)
            keep_warm(WARM)

            pe.wait_ge(s_pk, 16)
            mlp(0, pk[:, PK_C:PK_C + NB])
            for n in range(3):
                c = pk[:, PK_C:PK_C + NB] if n == 0 else pk[:, PK_C + n - 1:PK_C + n].to_broadcast([P, P])
                ins = pe.matmul(acc_b[0:NB if n == 0 else P, CH * n:CH * n + CH], c, pk[:, PK_CW:PK_CW + CH],
                                start=True, stop=True)
            ins.then_inc(ctx_mm, 1)
            pe.wait_ge(blk_loaded[0], 16)
            for n in range(2):
                for g in range(GROUPS):
                    if n == 0:
                        pe.wait_ge(s_filt[g], 16)
                    ins = conv_group(0, n, g)
                    if n == 0 and g == 1:
                        pe.wait_ge(mlp_h, 1)
                        mlp(1, hg[:, 0, :])
                ins.then_inc(mix_done, 1)
                if n == 0:
                    pe.wait_ge(mlp_h, 2)
                    pe.matmul(utp[0:NB, 2 * NB:2 * NB + KMIX], hg[:, 1, :], pk[:, PK_W2:PK_W2 + KMIX],
                              start=True, stop=True).then_inc(mlp_mm, 1)
            pe.wait_ge(consts, 3)
            pe.wait_ge(att_op, 5)
            pe.transpose(utp[:, 2 * P:2 * P + NB], att_rep[:, :, :].rearrange("b o k -> b (o k)"),
                         ident[0:NB, 0:NB]).then_inc(att_t, 1)
            keep_warm(WARM_WEIGHTS)

            pe.wait_ge(ctx_sum, 2)
            for k in range(NCH):
                if k % 4 == 0:
                    pe.wait_ge(acthi_done, 1 + k // 4)
                pe.wait_ge(whi_done, k + 1)
                for c in (PART_C, PART_A, PART_B):
                    a, b = COLS0[c]
                    pe.matmul(acc(c, 0)[:, 0:b - a], act_hi[:, 0, k, :], w_hi[:, k, a:b],
                              start=(k == 0), stop=False)
                pe.wait_ge(wlo_done, k + 1)
                for c in (PART_C, PART_A, PART_B):
                    a, b = COLS0[c]
                    dst = acc(c, 0)[:, 0:b - a]
                    pe.matmul(dst, act_hi[:, 0, k, :], w_lo[:, k, a:b], start=False, stop=False)
                    act_ready(0, k)
                    ins = pe.matmul(dst, act_lo[:, 0, k, :], w_hi[:, k, a:b], start=False,
                                    stop=(c == PART_C and k == NCH - 1))
                    if k == NCH - 1 and c == PART_C:
                        ins.then_inc(hid_done, 1)
                if k == 2:
                    pe.wait_ge(s_bk, 16)
                    pe.wait_ge(att_copied, 1)
                    pe.matmul(utp[0:NB, 3 * P:3 * P + CH], att_all[0:KMIX, :], bk[:, :],
                              start=True, stop=True).then_inc(aggb_mm, 1)
            pe.wait_ge(aggb_copied, 1)
            conv(1, 1, 0, between=lambda: turn_u(0, first=True))
            pe.wait_ge(s_mixw, 16)
            pe.wait_ge(att_diag_done, 2)
            for m in range(MIXES):
                half, at = m // (MIXES // 2), m % (MIXES // 2) * P
                if m == 0:
                    pe.wait_ge(sum_done, 3)
                ins = pe.matmul((mixp[:, 0, :], acc_a[:, 1, :])[half][:, at:at + P], mixw_sb[:, m, :],
                                att_diag[:, :, :].rearrange("p o t -> p (o t)"), start=True, stop=True)
                if at == BANK - P:
                    ins.then_inc(agg_mm, 1)
            pe.wait_ge(lblo_done, 1)
            pe.wait_ge(bias_split, 1)
            for c in (PART_C, PART_A, PART_B):
                lora0(0, 0, c)

            def step(T, s, pair, cols, lora, following, mixed_out=None):
                for k in range(NCH):
                    act_ready(T, k)
                    if k == 0:
                        if mixed_out is None:
                            pe.wait_ge(res_done[PART_C], T - 1)
                    ins = dense(s, cols, PART_C, k)
                ins.then_inc(hid_done, 1)
                if mixed_out is None:
                    pe.wait_ge(res_done[PART_A], T - 1)
                else:
                    pe.wait_ge(agg_read, mixed_out)
                for k in range(NCH):
                    dense(s, cols, PART_A, k)
                    if k == (NCH - 2 if following is not None else NCH - 4):
                        turn_u(T)
                if following is not None:
                    following(T + 1, 1 - s, pair + s)
                lora(T, s, PART_C)
                lora(T, s, PART_A)
                pe.wait_ge(res_done[PART_B], T)
                for k in range(NCH):
                    dense(s, cols, PART_B, k)
                lora(T, s, PART_B)

            def step0(T, s, pair, mixed_out=None):
                step(T, s, pair, COLS0, lora0, conv, mixed_out)

            def step1(T, s, pair):
                step(T, s, pair, COLS1, lora1, mix)

            step0(1, 1, 0, mixed_out=4)
            step0(2, 0, 1)
            loop_steps(pe, 3, TILES - 4, step0)
            T = TILES - 1
            for k in range(NCH):
                act_ready(T, k)
                if k == 0:
                    pe.wait_ge(res_done[PART_C], T - 1)
                ins = dense(1, COLS0, PART_C, k)
            ins.then_inc(hid_done, 1)
            mix(TILES, 0, TILES // 2)
            pe.wait_ge(res_done[PART_A], T - 1)
            pe.wait_ge(res_done[PART_B], T)
            for k in range(NCH):
                dense(1, COLS0, PART_A, k)
                dense(1, COLS0, PART_B, k).then_inc(w_free, 1)
                if k == 1:
                    turn_u(T)
            for c in (PART_C, PART_A, PART_B):
                lora0(T, 1, c)

            T = TILES
            pe.wait_ge(res_done[PART_C], T - 1)
            pe.wait_ge(res_done[PART_A], T - 1)
            for k in range(NCH):
                act_ready(T, k)
                pe.wait_ge(wlo_done, NCH + k + 1)
                for c in (PART_C, PART_A, PART_B):
                    if k == 0 and c == PART_B:
                        pe.wait_ge(res_done[PART_B], T)
                    ins = dense(0, COLS1, c, k)
                    if k == NCH - 1 and c == PART_C:
                        ins.then_inc(hid_done, 1)
            mix(T + 1, 1, T // 2, between=lambda: turn_u(T))
            pe.wait_ge(lblo_done, 2)
            for c in (PART_C, PART_A, PART_B):
                lora1(T, 0, c)

            loop_steps(pe, TILES + 1, TILES - 2, step1)
            step(LAST, 1, LAST // 2, COLS1, lora1, None)


_OUT = (NB, CH, D)


def _layout(inp):
    a = {k: np.asarray(v) for k, v in inp.items()}
    x = a["x"]
    xp = np.pad(x, ((0, 0), (0, 0), (PAD, PAD))).reshape(TILES, 2, GROUPS, GC, QX, POS)[..., ::-1]
    xblk = xp.transpose(0, 3, 5, 1, 2, 4).reshape(TILES, P, 2 * GROUPS * QX)
    toep = np.zeros((GROUPS, GC, TOEP, GC), np.float32)
    w = a["L0_cond_weight"].reshape(GROUPS, GC, GC, TAPS)[..., ::-1]
    toep[:, :, POS - 1:POS - 1 + TAPS, :] = w.transpose(0, 2, 3, 1)
    wcat0 = np.concatenate([a["L0_ffn_W"], a["L0_ffn_A"], a["L0_ffn_gate_w"]]).T.reshape(P, NCH, W0COLS)
    lora_a = a["L1_ffn_lora_A"].transpose(0, 2, 1).reshape(EXP * ER, D)
    wcat1 = np.concatenate([a["L1_ffn_W_base"], lora_a, a["L1_ffn_W_router"]]).T
    wcat1 = wcat1.reshape(NCH, P, W1COLS).transpose(1, 0, 2)
    bcat0 = np.concatenate([a["L0_ffn_B"].T, a["L0_ffn_B"].T])
    bias0 = np.zeros((ROWS0 - BIAS_HI, D), np.float32)
    bias0[0] = bias0[-1] = a["L0_ffn_b"]
    pack = np.concatenate([a["cond_128"].T, a["L0_cond_c_weight"].T, a["L1_cond_W0"], a["L1_cond_W1"],
                           a["L1_cond_W2"], a["L1_cond_b0"][:, None], a["L1_cond_b1"][:, None]], axis=1)
    rows = np.concatenate([a["fside_S_0"], a["L0_ffn_gate_b"], a["L1_cond_b2"], a["L1_ffn_b_router"]])
    mixw = np.zeros((2, OQ, KMIX, MIXES, 2, CH), np.float32)
    for n in range(2):
        mixw[n, :, :, :, n, :] = a["L1_cond_weight"].reshape(KMIX, MIXES, OQ, CH).transpose(2, 0, 1, 3)
    mixw = mixw.reshape(P, MIXES, 2 * CH)
    return {"x": x, "xblk": xblk, "toep": toep, "wcat0": wcat0, "bcat0": bcat0, "bias0": bias0, "wcat1": wcat1,
            "bcat1": a["L1_ffn_lora_B"].reshape(P, D), "b_base": a["L1_ffn_b_base"], "pack": pack, "rows": rows,
            "mixw": mixw, "bias_k": a["L1_cond_bias_k"]}


def kernel(**inputs):
    import concourse.bacc as bacc
    from concourse.bass_utils import run_bass_kernel_spmd

    nc = bacc.Bacc("TRN2", target_bir_lowering=False, num_devices=1)
    arrays, aps = {}, {}
    for name, a in _layout(inputs).items():
        a = np.ascontiguousarray(a)
        arrays[f"in_{name}"] = a
        aps[name] = nc.dram_tensor(f"in_{name}", a.shape, mybir.dt.from_np(a.dtype), kind="ExternalInput").ap()
    out = nc.dram_tensor("out_dram", _OUT, F32, kind="ExternalOutput").ap()
    build(nc, out=out, **aps)
    return run_bass_kernel_spmd(nc, [arrays], core_ids=[0]).results[0]["out_dram"]
```
